# Optimizing a Trainium2 kernel written in Bass

```python
import numpy as np
import jax
import jax.numpy as jnp

def _softmax(x, axis=-1):
    return jax.nn.softmax(x, axis=axis)

def _gelu(x):
    return jax.nn.gelu(x, approximate=True)

def _silu(x):
    return jax.nn.silu(x)

def _sigmoid(x):
    return jax.nn.sigmoid(x)

def _layernorm(x, axis=-1, eps=1e-05):
    m = jnp.mean(x, axis=axis, keepdims=True)
    v = jnp.var(x, axis=axis, keepdims=True)
    return (x - m) / jnp.sqrt(v + eps)

def _scatter_add(tgt, idx, src, axis=0):
    return tgt.at[idx].add(src)

def _segment_sum(src, seg, n):
    return jax.ops.segment_sum(src, seg, n)
kernel_name = 'mk_gnn_preln_d4_gnn_r32_ad7790'

def setup_inputs(seed: int=0):
    np.random.seed(seed)
    _w = jnp.asarray

    def _rec_inputs():
        import jax
        import jax.numpy as jnp
        _gk = jax.random.key(seed)
        x = -0.000202 + 1 * jax.random.normal(jax.random.fold_in(_gk, 1), (3125, 128), jnp.float32)
        src = jax.random.randint(jax.random.fold_in(_gk, 2), (100000,), 0, 3125, jnp.int32)
        dst = jax.random.randint(jax.random.fold_in(_gk, 3), (100000,), 0, 3125, jnp.int32)
        _o = jnp.argsort(dst, stable=True)
        src = src[_o]
        dst = dst[_o]
        edge_attr_42 = 0.000171677 + 1.0001 * jax.random.normal(jax.random.fold_in(_gk, 12), (100000, 42), jnp.float32)
        edge_type_8 = jax.random.randint(jax.random.fold_in(_gk, 14), (100000,), 0, 8, jnp.int32)
        edge_weight = jax.random.uniform(jax.random.fold_in(_gk, 15), (100000,), jnp.float32, 0.0, 1)
        node_vec = jax.random.uniform(jax.random.fold_in(_gk, 16), (3125,), jnp.float32, 0.0, 0.999994)
        return (x, src, dst, edge_attr_42, edge_type_8, edge_weight, node_vec)
    x, src, dst, edge_attr_42, edge_type_8, edge_weight, node_vec = _rec_inputs()

    def _L0_gnn_setup():
        import jax, jax.numpy as jnp
        import numpy as np
        N_NODES = 50000
        N_EDGES = 25000
        N_RELS = 8
        N_BASES = 4
        IN_FEAT = 128
        OUT_FEAT = 128
        key = jax.random.key(seed)
        k = jax.random.split(key, 7)
        x = jax.random.normal(k[0], (N_NODES, IN_FEAT), dtype=jnp.float32)
        edge_norm = jax.random.uniform(k[1], (N_EDGES,), dtype=jnp.float32)
        bases = jax.random.normal(k[2], (N_BASES, IN_FEAT, OUT_FEAT), dtype=jnp.float32) * 0.05
        w_comp = jax.random.normal(k[3], (N_RELS, N_BASES), dtype=jnp.float32)
        edge_src = jax.random.randint(k[4], (N_EDGES,), 0, N_NODES, dtype=jnp.int32)
        edge_dst = jax.random.randint(k[5], (N_EDGES,), 0, N_NODES, dtype=jnp.int32)
        edge_type = jax.random.randint(k[6], (N_EDGES,), 0, N_RELS, dtype=jnp.int32)
        return {'x': x, 'edge_norm': edge_norm, 'bases': bases, 'w_comp': w_comp, 'edge_src': edge_src, 'edge_dst': edge_dst, 'edge_type': edge_type}
    _L0_gnn_all = _L0_gnn_setup()
    _L0_gnn_in = {k: v for k, v in _L0_gnn_all.items() if k in ('bases', 'w_comp')}
    del _L0_gnn_all

    def _L1_gnn_setup():
        import jax, jax.numpy as jnp
        import numpy as np
        DIM = 128
        N_NODES = 3125
        N_EDGES = 20000
        key = jax.random.key(seed)
        k1, k2, k3, k4, k5, k6 = jax.random.split(key, 6)
        x = jax.random.normal(k1, (N_NODES, DIM), dtype=jnp.float32)
        edge_index = jax.random.randint(k2, (2, N_EDGES), 0, N_NODES, dtype=jnp.int64)
        edge_weight = jax.random.uniform(k3, (N_EDGES,), dtype=jnp.float32)
        bound = 1.0 / np.sqrt(DIM)
        W = jax.random.uniform(k4, (DIM, DIM), minval=-bound, maxval=bound, dtype=jnp.float32)
        b = jax.random.uniform(k5, (DIM,), minval=-bound, maxval=bound, dtype=jnp.float32)
        alpha = jnp.float32(0.5)
        return {'x': x, 'edge_index': edge_index, 'num_nodes': N_NODES, 'edge_weight': edge_weight, 'W': W, 'b': b, 'alpha': alpha}
    _L1_gnn_all = _L1_gnn_setup()
    _L1_gnn_in = {k: v for k, v in _L1_gnn_all.items() if k in ('W', 'b', 'alpha')}
    del _L1_gnn_all

    def _L2_gnn_setup():
        import jax, jax.numpy as jnp
        import numpy as np
        NODE_EMB_DIM = 16
        NUM_REL = 10

        def _rgcn_layer(x, src, dst, edge_type, w_rel, root, bias):
            N = x.shape[0]
            seg = dst * NUM_REL + edge_type
            xs = x[src]
            sums = jax.ops.segment_sum(xs, seg, num_segments=N * NUM_REL)
            cnt = jax.ops.segment_sum(jnp.ones(seg.shape, x.dtype), seg, num_segments=N * NUM_REL)
            mean = (sums / jnp.maximum(cnt, 1.0)[:, None]).reshape(N, NUM_REL, -1)
            return jnp.einsum('nrd,rdo->no', mean, w_rel) + x @ root + bias
        key = jax.random.key(seed)
        ks = jax.random.split(key, 10)
        N, E, C = (50000, 25000, 128)
        s = 1.0 / np.sqrt(C).astype(np.float32)
        x = jax.random.normal(ks[0], (N, C), jnp.float32)
        last_update = jax.random.uniform(ks[1], (N,), jnp.float32)
        t = jax.random.uniform(ks[2], (E,), jnp.float32)
        msg = jax.random.normal(ks[3], (E, 2 * NODE_EMB_DIM + NUM_REL), jnp.float32)
        w_rel1 = jax.random.normal(ks[4], (NUM_REL, C, C), jnp.float32) * s
        root1 = jax.random.normal(ks[5], (C, C), jnp.float32) * s
        b1 = jnp.zeros((C,), jnp.float32)
        w_rel2 = jax.random.normal(ks[6], (NUM_REL, C, C), jnp.float32) * s
        root2 = jax.random.normal(ks[7], (C, C), jnp.float32) * s
        b2 = jnp.zeros((C,), jnp.float32)
        edge_index = jax.random.randint(ks[8], (2, E), 0, N, dtype=jnp.int32)
        return dict(x=x, last_update=last_update, t=t, msg=msg, w_rel1=w_rel1, root1=root1, b1=b1, w_rel2=w_rel2, root2=root2, b2=b2, edge_index=edge_index)
    _L2_gnn_all = _L2_gnn_setup()
    _L2_gnn_in = {k: v for k, v in _L2_gnn_all.items() if k in ('w_rel1', 'root1', 'b1', 'w_rel2', 'root2', 'b2')}
    del _L2_gnn_all

    def _L3_gnn_setup():
        import jax, jax.numpy as jnp
        import numpy as np
        N = 3125
        E = 50000
        D_IN = 128
        D_OUT = 128
        key = jax.random.key(seed)
        k1, k2, k3, k4, k5 = jax.random.split(key, 5)
        x = jax.random.normal(k1, (N, D_IN), dtype=jnp.float32)
        edge_index = jax.random.randint(k2, (2, E), 0, N, dtype=jnp.int32)
        bound = 1.0 / np.sqrt(D_IN)
        W_rel = jax.random.uniform(k3, (D_OUT, D_IN), minval=-bound, maxval=bound, dtype=jnp.float32)
        b_rel = jax.random.uniform(k4, (D_OUT,), minval=-bound, maxval=bound, dtype=jnp.float32)
        W_root = jax.random.uniform(k5, (D_OUT, D_IN), minval=-bound, maxval=bound, dtype=jnp.float32)
        return {'x': x, 'res_size': N, 'edge_index': edge_index, 'W_rel': W_rel, 'b_rel': b_rel, 'W_root': W_root}
    _L3_gnn_all = _L3_gnn_setup()
    _L3_gnn_in = {k: v for k, v in _L3_gnn_all.items() if k in ('W_rel', 'b_rel', 'W_root')}
    del _L3_gnn_all
    return {'x': x, 'src': src, 'dst': dst, 'edge_attr_42': edge_attr_42, 'edge_type_8': edge_type_8, 'edge_weight': edge_weight, 'node_vec': node_vec, 'L0_gnn_bases': _L0_gnn_in['bases'], 'L0_gnn_w_comp': _L0_gnn_in['w_comp'], 'L1_gnn_W': _L1_gnn_in['W'], 'L1_gnn_b': _L1_gnn_in['b'], 'L1_gnn_alpha': _L1_gnn_in['alpha'], 'L2_gnn_w_rel1': _L2_gnn_in['w_rel1'], 'L2_gnn_root1': _L2_gnn_in['root1'], 'L2_gnn_b1': _L2_gnn_in['b1'], 'L2_gnn_w_rel2': _L2_gnn_in['w_rel2'], 'L2_gnn_root2': _L2_gnn_in['root2'], 'L2_gnn_b2': _L2_gnn_in['b2'], 'L3_gnn_W_rel': _L3_gnn_in['W_rel'], 'L3_gnn_b_rel': _L3_gnn_in['b_rel'], 'L3_gnn_W_root': _L3_gnn_in['W_root']}

def reference(x, src, dst, edge_attr_42, edge_type_8, edge_weight, node_vec, L0_gnn_bases, L0_gnn_w_comp, L1_gnn_W, L1_gnn_b, L1_gnn_alpha, L2_gnn_w_rel1, L2_gnn_root1, L2_gnn_b1, L2_gnn_w_rel2, L2_gnn_root2, L2_gnn_b2, L3_gnn_W_rel, L3_gnn_b_rel, L3_gnn_W_root):
    import jax
    import jax.numpy as jnp

    def _L0_gnn_ref(x, edge_norm, bases, w_comp, edge_src, edge_dst, edge_type):
        import jax, jax.numpy as jnp
        import numpy as np
        N_NODES = 50000
        N_EDGES = 25000
        N_RELS = 8
        N_BASES = 4
        IN_FEAT = 128
        OUT_FEAT = 128
        N = x.shape[0]
        R = w_comp.shape[0]
        W = jnp.einsum('rb,bio->rio', w_comp, bases)
        msg = x[edge_src] * edge_norm[:, None]
        seg = edge_type * N + edge_dst
        agg = jax.ops.segment_sum(msg, seg, num_segments=R * N)
        agg = agg.reshape(R, N, -1)
        out = jnp.einsum('rni,rio->no', agg, W)
        return out

    def _L1_gnn_ref(x, edge_index, num_nodes, edge_weight, W, b, alpha):
        import jax, jax.numpy as jnp
        import numpy as np
        DIM = 128
        N_NODES = 3125
        N_EDGES = 20000
        src = edge_index[0]
        dst = edge_index[1]
        msg = x[src] * edge_weight[:, None]
        agg = jax.ops.segment_sum(msg, dst, num_segments=num_nodes)
        deg = jax.ops.segment_sum(jnp.ones_like(edge_weight), dst, num_segments=num_nodes)
        deg = jnp.maximum(deg, 1.0)
        agg = agg / deg[:, None]
        return x + alpha * (agg @ W.T + b)

    def _L2_gnn_ref(x, last_update, t, msg, w_rel1, root1, b1, w_rel2, root2, b2, edge_index):
        import jax, jax.numpy as jnp
        import numpy as np
        NODE_EMB_DIM = 16
        NUM_REL = 10

        def _rgcn_layer(x, src, dst, edge_type, w_rel, root, bias):
            N = x.shape[0]
            seg = dst * NUM_REL + edge_type
            xs = x[src]
            sums = jax.ops.segment_sum(xs, seg, num_segments=N * NUM_REL)
            cnt = jax.ops.segment_sum(jnp.ones(seg.shape, x.dtype), seg, num_segments=N * NUM_REL)
            mean = (sums / jnp.maximum(cnt, 1.0)[:, None]).reshape(N, NUM_REL, -1)
            return jnp.einsum('nrd,rdo->no', mean, w_rel) + x @ root + bias
        src, dst = (edge_index[0], edge_index[1])
        edge_type = jnp.argmax(msg[:, NODE_EMB_DIM:-NODE_EMB_DIM], axis=1).astype(jnp.int32)
        h = jax.nn.relu(_rgcn_layer(x, src, dst, edge_type, w_rel1, root1, b1))
        return _rgcn_layer(h, src, dst, edge_type, w_rel2, root2, b2)

    def _L3_gnn_ref(x, res_size, edge_index, W_rel, b_rel, W_root):
        import jax, jax.numpy as jnp
        import numpy as np
        N = 3125
        E = 50000
        D_IN = 128
        D_OUT = 128
        row, col = (edge_index[0], edge_index[1])
        msg_sum = jax.ops.segment_sum(x[row], col, num_segments=res_size)
        cnt = jax.ops.segment_sum(jnp.ones((row.shape[0],), dtype=x.dtype), col, num_segments=res_size)
        mean = msg_sum / jnp.maximum(cnt, 1.0)[:, None]
        out = mean @ W_rel.T + b_rel + x[:res_size] @ W_root.T
        norm = jnp.linalg.norm(out, axis=-1, keepdims=True)
        return out / jnp.maximum(norm, 1e-12)
    edge_index = jnp.stack([src, dst])
    h = jnp.maximum(_layernorm(x, axis=-1), 0.0)
    x = x + _L0_gnn_ref(h, edge_weight, L0_gnn_bases, L0_gnn_w_comp, src, dst, edge_type_8)
    h = jnp.maximum(_layernorm(x, axis=-1), 0.0)
    x = x + _L1_gnn_ref(h, edge_index, 3125, edge_weight, L1_gnn_W, L1_gnn_b, L1_gnn_alpha)
    h = jnp.maximum(_layernorm(x, axis=-1), 0.0)
    x = x + _L2_gnn_ref(h, node_vec, edge_weight, edge_attr_42, L2_gnn_w_rel1, L2_gnn_root1, L2_gnn_b1, L2_gnn_w_rel2, L2_gnn_root2, L2_gnn_b2, edge_index)
    h = jnp.maximum(_layernorm(x, axis=-1), 0.0)
    x = x + _L3_gnn_ref(h, 3125, edge_index, L3_gnn_W_rel, L3_gnn_b_rel, L3_gnn_W_root)
    return x

_drawn_inputs = setup_inputs


def setup_inputs(seed=0):
    import zlib

    import numpy as np

    out = dict(_drawn_inputs(seed))
    spreads = {'L2_gnn_b1': (0.0, 0.1), 'L2_gnn_b2': (0.0, 0.531)}
    factors = {'L1_gnn_W': 3.409,
     'L1_gnn_b': 8.0,
     'L3_gnn_W_rel': 6.413,
     'L3_gnn_b_rel': 8.0,
     'L3_gnn_W_root': 5.157}
    for name, (base, spread) in spreads.items():
        noise = np.random.default_rng([zlib.crc32(name.encode()), seed]).standard_normal(out[name].shape)
        drawn = base * np.exp(spread * noise) if base else spread * noise
        out[name] = jnp.asarray(drawn.astype(out[name].dtype))
    for name, factor in factors.items():
        out[name] = (out[name] * factor).astype(out[name].dtype)
    return out
```

```python
import concourse.bass as bass
from concourse import mybir
from contextlib import ExitStack

F32 = mybir.dt.float32
BF16 = mybir.dt.bfloat16
I32 = mybir.dt.int32
ALU = mybir.AluOpType
ACT = mybir.ActivationFunctionType
X = mybir.AxisListType.X

P = 128
F = 128
WIN = 16
GT = 2
RING = 8
OHRING = 4
BANKS = 4
HALF = 4
LAG = 2
R0 = 8
NBASES = 4
R2 = 10
EMB = 16
CHUNK = 512
PAD_DST = 4096
LN_EPS = 1e-5
NORM_EPS = 1e-12
PASSES = 5
RELS = [R0, 1, R2, R2, 1]
WEIGHTED = [True, True, False, False, False]


def graph_layers(nc, x_in, src_in, dst_in, base_in, type8_in, logit_in, w_in, comp_in, bases_in,
                 w1t_in, b1_in, alpha_in, wrel_a_in, root_a_in, bias_a_in, wrel_b_in, root_b_in, bias_b_in,
                 w3rel_in, b3_in, w3root_in, out):
    N = x_in.shape[0]
    NT = src_in.shape[1]
    NG = NT // GT
    ITER = NG // RING
    NB = -(-N // P)
    NFULL = N // P
    NREST = N - NFULL * P
    NA = N + WIN
    NC = -(-N // CHUNK)
    BATCH = 5
    NBATCH = NB // BATCH
    assert NB % BATCH == 0 and NG % RING == 0 and NREST > 0 and PAD_DST >= NC * CHUNK

    def rows(b):
        return P if b < NFULL else NREST

    table = nc.dram_tensor("node_table", [N, F], F32).ap()

    ctx = ExitStack()
    with ctx:
        def sb(name, shape, dt=F32):
            return ctx.enter_context(nc.sbuf_tensor(name, shape, dt))

        def sem(name):
            return ctx.enter_context(nc.semaphore(name))

        agg = sb("agg", [P, R2 * NA])
        x = sb("x", [P, NB, F])
        hb = sb("hb", [P, NB, F])
        src = sb("src", [P, NT], I32)
        weight = sb("weight", [P, NT])
        local = sb("local", [P, NT])
        key = sb("key", [P, NT])
        type10 = sb("type10", [P, NT])
        bases_row = sb("bases_row", [1, NG], I32)
        stage = sb("stage", [P, 2, HALF * GT], I32)
        work = sb("work", [P, 4096])
        msg = work[:, 0:RING * GT * F].rearrange("p (s f) -> p s f", f=F)
        oh = work[:, RING * GT * F:RING * GT * F + OHRING * GT * R2 * WIN].rearrange(
            "p (s c) -> p s c", c=R2 * WIN)
        g_msg = work[:, 0:F]
        wide = work[:, F:F + NC * CHUNK].rearrange("p (c n) -> p c n", n=CHUNK)
        g_types = sb("g_types", [P, R2])
        g_coef = sb("g_coef", [P, 1])
        g_key = sb("g_key", [P, NC])
        starts = sb("starts", [P, NC])
        down = sb("down", [P, R2])
        adeg = sb("adeg", [P, NB])
        t_oh = sb("t_oh", [P, 2, HALF * GT, R2], BF16)
        n_oh = sb("n_oh", [P, 2, HALF * GT, WIN], BF16)
        wts = sb("wts", [P, R2, F])
        root = sb("root", [P, F])
        bias = sb("bias", [P, F])
        hT = sb("hT", [P, 2, P])
        ident = sb("ident", [P, P])
        iota = sb("iota", [P, CHUNK])
        comp = sb("comp", [P, R0 * NBASES])
        alpha = sb("alpha", [P, 1])
        eps = sb("eps", [P, 1])
        rel = sb("rel", [P, 1])
        inv10 = sb("inv10", [P, NB, R2])
        invdeg = sb("invdeg", [P, NB])
        stats = sb("stats", [P, BATCH, 6])
        mv = sb("mv", [P, NB, 2])
        rstd = sb("rstd", [P, NB])
        shift = sb("shift", [P, NB])
        good = sb("good", [P, 1])
        ones = sb("ones", [P, 1])
        flag = sb("flag", [1, 1], I32)
        bank = [ctx.enter_context(nc.psum_tensor(f"bank{i}", [P, CHUNK], F32)) for i in range(8)]

        col = [0]

        def carve(n, dt=F32):
            a = agg[:, col[0]:col[0] + n]
            col[0] += n
            return a if dt == F32 else a.bitcast(dt)

        logits = carve(NT * R2).rearrange("p (t r) -> p t r", r=R2)
        firsts = carve(NT * R2).rearrange("p (t r) -> p t r", r=R2)
        dst_i = carve(NT, I32)
        type8_i = carve(NT, I32)
        base_i = carve(NG, I32)
        dst_f = carve(NT)
        type8_f = carve(NT)
        base_f = carve(NG)
        top = carve(NT)
        spare = carve(NT)
        basis = carve(NBASES * F).rearrange("p (b f) -> p b f", f=F)
        counts = agg[0:R2, R0 * NA:(R0 + 1) * NA]

        def by_relation(n):
            return agg[:, 0:n * NA].rearrange("p (r n) -> p r n", n=NA)

        loaded = sem("loaded")
        wload = [sem(f"wload{k}") for k in range(PASSES)]
        prep = sem("prep")
        pool_prep = sem("pool_prep")
        good_ready = sem("good_ready")
        flag_sum = sem("flag_sum")
        flag_ok = sem("flag_ok")
        stats_ready = sem("stats_ready")
        std_ready = sem("std_ready")
        scale_ready = sem("scale_ready")
        h_ready = sem("h_ready")
        table_ready = sem("table_ready")
        agg_ready = sem("agg_ready")
        tr_done = sem("tr_done")
        tr_used = sem("tr_used")
        rt_T = sem("rt_T")
        rt_c = sem("rt_c")
        rt_mm = sem("rt_mm")
        rt_used = sem("rt_used")
        cnt_T = sem("cnt_T")
        cnt_used = sem("cnt_used")
        x_ready = sem("x_ready")
        out_sem = sem("out_sem")
        idx_ready = sem("idx_ready")
        gathered = [sem(f"gathered{s}") for s in range(RING * GT)]
        oh_ready = sem("oh_ready")
        seg_done = sem("seg_done")
        acc_done = sem("acc_done")
        pool_go = sem("pool_go")
        g_idx = sem("g_idx")
        g_gathered = sem("g_gathered")
        g_step = sem("g_step")
        g_rel = sem("g_rel")
        g_oh = sem("g_oh")
        g_seg = sem("g_seg")

        step = [0]

        def link(ins):
            step[0] += 1
            ins.then_inc(prep, 1)
            nc.vector.wait_ge(prep, step[0])

        def mark(ins):
            step[0] += 1
            ins.then_inc(prep, 1)

        def meet():
            nc.vector.wait_ge(prep, step[0])

        ROUNDS, before = [], 0
        for k, relations in [(0, 1)] + list(enumerate(RELS)):
            ROUNDS.append((k, relations, before))
            before += relations * NT

        block = ctx.enter_context(nc.Block())

        TABLE_DMAS = NBATCH + 1

        def store_rows(sp, dram, batch, tile, semaphore):
            b0, b1 = batch * BATCH, min((batch + 1) * BATCH, NFULL)
            sp.dma_start(dram[b0 * P:b1 * P, :].rearrange("(b p) f -> p b f", p=P),
                         tile[:, b0:b1, :]).then_inc(semaphore, 16)
            if batch == NBATCH - 1:
                sp.dma_start(dram[NFULL * P:N, :], tile[0:NREST, NFULL, :]).then_inc(semaphore, 16)

        def load_weights(sp, k):
            if k:
                sp.wait_ge(tr_used, k * NB)
            w_src, r_src, b_src = [(None, None, None), (w1t_in, None, b1_in),
                                   (wrel_a_in, root_a_in, bias_a_in), (wrel_b_in, root_b_in, bias_b_in),
                                   (w3rel_in, w3root_in, b3_in)][k]
            n = RELS[k]
            sp.dma_start(wts[:, 0:n, :], w_src.rearrange("(r d) f -> d r f", d=F)).then_inc(wload[k], 16)
            if r_src is not None:
                sp.dma_start(root[:, :], r_src).then_inc(wload[k], 16)
            sp.dma_start(bias[:, :], b_src.partition_broadcast(P)).then_inc(wload[k], 16)

        def sp_path(sp):
            for k in range(PASSES):
                for batch in range(NBATCH):
                    sp.wait_ge(h_ready, k * NBATCH + batch + 1)
                    store_rows(sp, table, batch, hb, table_ready)
                if k:
                    load_weights(sp, k)
            for batch in range(NBATCH):
                sp.wait_ge(x_ready, batch + 1)
                store_rows(sp, out, batch, x, out_sem)
            sp.wait_ge(out_sem, 16 * TABLE_DMAS)

        @block.sync
        def _(sp):
            sp.dma_start(dst_i, dst_in).then_inc(loaded, 16)
            sp.dma_start(base_i, base_in.partition_broadcast(P)).then_inc(loaded, 16)
            sp.dma_start(x[:, 0:NFULL, :], x_in[0:NFULL * P, :].rearrange("(b p) f -> p b f", p=P)
                         ).then_inc(loaded, 16)
            sp.dma_start(x[0:NREST, NFULL, :], x_in[NFULL * P:N, :]).then_inc(loaded, 16)
            sp.dma_start(bases_row[:, :], base_in.rearrange("(o g) -> o g", o=1)).then_inc(loaded, 16)
            sp.dma_start(type8_i, type8_in).then_inc(loaded, 16)
            sp.dma_start(weight[:, :], w_in).then_inc(loaded, 16)
            sp.dma_start(src[:, :], src_in).then_inc(loaded, 16)
            sp.dma_start(logits, logit_in).then_inc(loaded, 16)
            sp.dma_start(basis, bases_in.rearrange("b d f -> d b f")).then_inc(loaded, 16)
            sp.dma_start(comp[:, :], comp_in.partition_broadcast(P)).then_inc(loaded, 16)
            sp.dma_start(alpha[:, :], alpha_in.partition_broadcast(P)).then_inc(loaded, 16)
            sp.wait_ge(flag_ok, 1)
            fast = sp.value_load(flag[0:1, 0:1], min_val=0, max_val=1)
            with sp.If(fast > 0):
                sp_path(sp)
            with sp.Else():
                sp_path(sp)
            sp.nop()

        LOADS = 12

        def gather(pool, dst, index):
            return pool.indirect_dma_start(dst, None, table, bass.IndirectOffsetOnAxis(ap=index, axis=0))

        def pool_fast(pool):
            for k in range(PASSES):
                pool.wait_ge(table_ready, 16 * TABLE_DMAS * (k + 1))
                with pool.Fori(0, ITER) as i:
                    for u in range(RING):
                        if u % HALF == 0:
                            pool.wait_ge(idx_ready, 2 * i + (k * 2 * ITER + u // HALF + 1))
                        pool.wait_ge(seg_done, RING * i + (k * NG + u + 1))
                        pool.sem_inc(pool_go, 1)
                        for j in range(GT):
                            s = u * GT + j
                            gather(pool, msg[:, s, :],
                                   stage[:, u // HALF, s % (HALF * GT):s % (HALF * GT) + 1]
                                   ).then_inc(gathered[s], 16)

        def pool_general(pool):
            for n, (k, relations, before) in enumerate(ROUNDS):
                if n != 1:
                    pool.wait_ge(table_ready, 16 * TABLE_DMAS * (k + 1))
                    pool.sem_inc(pool_go, 1)
                with pool.Fori(0, relations * NT) as t:
                    pool.wait_ge(g_idx, t + (before + 1))
                    pool.sem_inc(pool_go, 1)
                    gather(pool, g_msg, stage[:, 0, 0:1]).then_inc(g_gathered, 16)

        @block.gpsimd
        def _(pool):
            pool.iota(iota[:, :], [[1, CHUNK]], base=0, channel_multiplier=0,
                      allow_small_or_imprecise_dtypes=True).then_inc(pool_prep, 1)
            pool.memset(ident[:, :], 0.0).then_inc(pool_prep, 1)
            pool.wait_ge(pool_prep, 2)
            pool.affine_select(out=ident[:, :], in_=ident[:, :], compare_op=ALU.not_equal, fill=1.0,
                               base=0, pattern=[[-1, P]], channel_multiplier=1).then_inc(pool_prep, 1)
            pool.wait_ge(flag_ok, 1)
            fast = pool.value_load(flag[0:1, 0:1], min_val=0, max_val=1)
            with pool.If(fast > 0):
                pool_fast(pool)
            with pool.Else():
                pool_general(pool)
            pool.nop()

        def act_normalise(act, n, k):
            for batch in range(NBATCH):
                b0 = batch * BATCH
                act.wait_ge(stats_ready, n * NBATCH + batch + 1)
                act.activation(rstd[:, b0:b0 + BATCH], mv[:, b0:b0 + BATCH, 1], ACT.Sqrt,
                               bias=eps[:, :]).then_inc(std_ready, 1)
                act.wait_ge(scale_ready, n * NBATCH + batch + 1)
                if k:
                    act.wait_ge(table_ready, 16 * TABLE_DMAS * k)
                for b in range(b0, b0 + BATCH):
                    m = rows(b)
                    last = act.activation(hb[0:m, b, :], x[0:m, b, :], ACT.Relu,
                                          bias=shift[0:m, b:b + 1], scale=rstd[0:m, b:b + 1])
                last.then_inc(h_ready, 1)

        def act_rectify(act, k):
            for batch in range(NBATCH):
                for b in range(batch * BATCH, (batch + 1) * BATCH):
                    m = rows(b)
                    act.wait_ge(tr_used, (k - 1) * NB + b + 1)
                    last = act.activation(hb[0:m, b, :], hb[0:m, b, :], ACT.Relu)
                last.then_inc(h_ready, 1)

        def act_root(act, n):
            for b in range(NB):
                m = rows(b)
                act.wait_ge(rt_T, n * NB + b + 1)
                act.activation(hT[:, b % 2, 0:m], bank[4 + b % 2][:, 0:m], ACT.Copy).then_inc(rt_c, 1)

        def act_stage_indices(act, k):
            with act.Fori(0, ITER) as i:
                for h in range(2):
                    act.wait_ge(seg_done, RING * i + (k * NG + HALF * (h + 1)))
                    act.activation(stage[:, h, :], src[:, bass.ds(RING * GT * i + h * HALF * GT, HALF * GT)],
                                   ACT.Copy).then_inc(idx_ready, 1)

        def act_stage_general(act, k):
            for _, relations, before in [x for x in ROUNDS if x[0] == k]:
                with act.Fori(0, relations) as r:
                    with act.Fori(0, NT) as t:
                        act.wait_ge(g_seg, r * NT + t + (before + 1))
                        act.activation(stage[:, 0, 0:1], src[:, bass.ds(t, 1)], ACT.Copy).then_inc(g_idx, 1)

        def act_path(act, fast):
            norms = roots = 0
            for k in range(PASSES):
                if k == 3:
                    act_rectify(act, k)
                else:
                    act_normalise(act, norms, k)
                    norms += 1
                if k >= 2:
                    act_root(act, roots)
                    roots += 1
                if fast:
                    act_stage_indices(act, k)
                else:
                    act_stage_general(act, k)
            for batch in range(NBATCH):
                b0 = batch * BATCH
                act.wait_ge(stats_ready, norms * NBATCH + batch + 1)
                act.activation(rstd[:, b0:b0 + BATCH], shift[:, b0:b0 + BATCH], ACT.Sqrt).then_inc(std_ready, 1)

        @block.scalar
        def _(act):
            act.wait_ge(flag_ok, 1)
            fast = act.value_load(flag[0:1, 0:1], min_val=0, max_val=1)
            with act.If(fast > 0):
                act_path(act, True)
            with act.Else():
                act_path(act, False)
            act.nop()

        def pe_root(pe, n, k):
            pe.wait_ge(wload[k], 16 * 3)
            for b in range(NB + 1):
                if b < NB:
                    m = rows(b)
                    pe.wait_ge(h_ready, k * NBATCH + b // BATCH + 1)
                    if n * NB + b >= 2:
                        pe.wait_ge(rt_c, n * NB + b - 1)
                    pe.transpose(bank[4 + b % 2][:, 0:m], hb[0:m, b, :], ident[0:m, 0:m]).then_inc(rt_T, 1)
                if b >= 1:
                    c = b - 1
                    m = rows(c)
                    pe.wait_ge(rt_c, n * NB + c + 1)
                    if n * NB + c >= 2:
                        pe.wait_ge(rt_used, n * NB + c - 1)
                    pe.matmul(bank[6 + c % 2][0:m, 0:F], hT[:, c % 2, 0:m], root[:, :],
                              start=True, stop=True).then_inc(rt_mm, 1)

        def pe_sum_groups(pe, k):
            n = RELS[k] * WIN
            if k == 0:
                pe.sem_inc(seg_done, RING)
            with pe.Fori(0, ITER) as i:
                for u in range(RING):
                    ps = bank[u % BANKS]
                    pe.wait_ge(oh_ready, RING * i + (k * NG + u + 1))
                    pe.wait_ge(acc_done, RING * i + (k * (NG + 1) + u + 2))
                    for j in range(GT):
                        s = u * GT + j
                        pe.wait_ge(gathered[s], 16 * i + 16 * (k * ITER + 1))
                        last = pe.matmul(ps[:, 0:n], msg[:, s, :], oh[:, s % (OHRING * GT), 0:n],
                                         start=(j == 0), stop=(j == GT - 1))
                    if k == 0:
                        for j in range(GT):
                            s = u * GT + j
                            v = s % (HALF * GT)
                            last = pe.matmul(ps[0:R2, n:n + WIN], t_oh[:, u // HALF, v, :],
                                             n_oh[:, u // HALF, v, :], start=(j == 0), stop=(j == GT - 1))
                    last.then_inc(seg_done, 1)

        def pe_sum_general(pe, k):
            for n, (kk, relations, before) in enumerate(ROUNDS):
                if kk != k:
                    continue
                m = R2 if n == 0 else P
                a = g_types[:, :] if n == 0 else g_msg

                def tile(r, t, start, stop):
                    pe.wait_ge(g_oh, r * NT + t + (before + 1))
                    pe.wait_ge(g_gathered, (r * NT + t) * 16 + 16 * (before + 1))
                    for c in range(NC):
                        last = pe.matmul(bank[c][0:m, :], a, wide[:, c, :], start=start, stop=stop)
                    last.then_inc(g_seg, 1)

                with pe.Fori(0, relations) as r:
                    tile(r, 0, True, False)
                    with pe.Fori(1, NT - 1) as t:
                        tile(r, t, False, False)
                    tile(r, NT - 1, False, True)

        def pe_transform(pe, k):
            aggs = by_relation(RELS[k])
            pe.wait_ge(agg_ready, k + 1)
            if k == 1:
                pe.wait_ge(wload[k], 16 * 2)
            for b in range(NB):
                m, n0 = rows(b), b * P
                if RELS[k] == R2:
                    if k * NB + b >= 2:
                        pe.wait_ge(tr_used, k * NB + b - 1)
                    for r in range(R2):
                        last = pe.matmul(bank[3 * (b % 2) + r // 4][0:m, (r % 4) * F:(r % 4 + 1) * F],
                                         aggs[:, r, n0:n0 + m], wts[:, r, :], start=True, stop=True)
                else:
                    if k * NB + b >= 2:
                        pe.wait_ge(tr_used, k * NB + b - 1)
                    for r in range(RELS[k]):
                        last = pe.matmul(bank[b % 2][0:m, 0:F], aggs[:, r, n0:n0 + m], wts[:, r, :],
                                         start=(r == 0), stop=(r == RELS[k] - 1))
                last.then_inc(tr_done, 1)
            if k == 0:
                for b in range(NB):
                    m = rows(b)
                    last = pe.transpose(bank[7][0:m, b * R2:(b + 1) * R2], counts[:, b * P:b * P + m],
                                        ident[0:R2, 0:R2])
                last.then_inc(cnt_T, 1)

        def pe_path(pe, fast):
            roots = 0
            if not fast:
                pe.sem_inc(g_seg, 1)
            for k in range(PASSES):
                if k >= 2:
                    pe_root(pe, roots, k)
                    roots += 1
                if fast:
                    pe_sum_groups(pe, k)
                else:
                    pe_sum_general(pe, k)
                pe_transform(pe, k)

        @block.tensor
        def _(pe):
            pe.wait_ge(good_ready, 1)
            pe.matmul(bank[7][0:1, 0:1], good[:, :], ones[:, :], start=True, stop=True).then_inc(flag_sum, 1)
            pe.wait_ge(flag_ok, 1)
            fast = pe.value_load(flag[0:1, 0:1], min_val=0, max_val=1)
            with pe.If(fast > 0):
                pe_path(pe, True)
            with pe.Else():
                pe_path(pe, False)
            pe.nop()

        def dve_stats(dve, n, batch):
            b0 = batch * BATCH
            for b in range(b0, b0 + BATCH):
                m = rows(b)
                mark(dve.bn_stats(stats[0:m, b - b0, :], x[0:m, b, :]))
            meet()
            for b in range(b0, b0 + BATCH):
                m = rows(b)
                last = dve.bn_aggr(mv[0:m, b, :], stats[0:m, b - b0, :])
            last.then_inc(stats_ready, 1)
            dve.wait_ge(std_ready, n * NBATCH + batch + 1)
            link(dve.reciprocal(rstd[:, b0:b0 + BATCH], rstd[:, b0:b0 + BATCH]))
            dve.scalar_tensor_tensor(shift[:, b0:b0 + BATCH], mv[:, b0:b0 + BATCH, 0], -1.0,
                                     rstd[:, b0:b0 + BATCH], ALU.mult, ALU.mult).then_inc(scale_ready, 1)

        def dve_root(dve, n, k):
            dve.wait_ge(wload[k], 16 * 3)
            dve.wait_ge(table_ready, 16 * TABLE_DMAS * (k + 1))
            for b in range(NB):
                m = rows(b)
                dve.wait_ge(rt_mm, n * NB + b + 1)
                ps = bank[6 + b % 2][0:m, 0:F]
                if k == 3:
                    ins = dve.tensor_tensor(x[0:m, b, :], x[0:m, b, :], ps, ALU.add)
                    ins.then_inc(rt_used, 1)
                    dve.wait_ge(rt_used, n * NB + b + 1)
                    mark(dve.tensor_tensor(x[0:m, b, :], x[0:m, b, :], bias[0:m, :], ALU.add))
                else:
                    dve.tensor_tensor(hb[0:m, b, :], ps, bias[0:m, :], ALU.add).then_inc(rt_used, 1)
            meet()
            dve.wait_ge(rt_used, (n + 1) * NB)

        def dve_sum_groups(dve, k):
            n = RELS[k] * WIN
            keys = local if RELS[k] == 1 else key
            aggs = by_relation(RELS[k])
            if k == 0:
                mark(dve.memset(counts, 0.0))
                dve.sem_inc(acc_done, BANKS)
            dve.memset(agg[:, 0:RELS[k] * NA], 0.0).then_inc(acc_done, 1)

            def build(g, slot):
                if k == 0 and slot % HALF == 0:
                    h = (slot // HALF) % 2
                    tiles = HALF * GT
                    dve.wait_ge(seg_done, g + HALF)
                    dve.tensor_tensor(n_oh[:, h, :, :], iota[:, 0:WIN].unsqueeze(1).broadcast_to([P, tiles, WIN]),
                                      local[:, bass.ds(GT * g, tiles)].unsqueeze(2).broadcast_to([P, tiles, WIN]),
                                      ALU.is_equal)
                    dve.tensor_tensor(t_oh[:, h, :, :], iota[:, 0:R2].unsqueeze(1).broadcast_to([P, tiles, R2]),
                                      type10[:, bass.ds(GT * g, tiles)].unsqueeze(2).broadcast_to([P, tiles, R2]),
                                      ALU.is_equal)
                dve.wait_ge(seg_done, g + (k * NG + RING - OHRING + 1))
                for j in range(GT):
                    c = bass.ds(GT * g + j, 1)
                    o = oh[:, (slot * GT + j) % (OHRING * GT), 0:n]
                    if WEIGHTED[k]:
                        last = dve.tensor_scalar(o, iota[:, 0:n], keys[:, c], weight[:, c],
                                                 ALU.is_equal, ALU.mult)
                    else:
                        last = dve.tensor_scalar(o, iota[:, 0:n], keys[:, c], None, ALU.is_equal)
                last.then_inc(oh_ready, 1)

            def add(g, slot):
                base = dve.value_load(bases_row[0:1, bass.ds(g, 1)], min_val=0, max_val=N - 1)
                dve.wait_ge(seg_done, g + (k * NG + RING + 1))
                dve.wait_ge(acc_done, g + (k * (NG + 1) + BANKS + 1))
                ps = bank[slot % BANKS]
                win = aggs[:, :, bass.ds(base, WIN)]
                if k == 0:
                    c = counts[:, bass.ds(base, WIN)]
                    dve.tensor_tensor(c, c, ps[0:R2, n:n + WIN], ALU.add)
                dve.tensor_tensor(win, win, ps[:, 0:n].rearrange("p (r n) -> p r n", n=WIN),
                                  ALU.add).then_inc(acc_done, 1)

            def turns(i, builds):
                for u in range(RING):
                    if u + LAG < builds:
                        build(RING * i + u + LAG, u + LAG)
                    add(RING * i + u, u)

            if k == 0:
                meet()
            for g in range(LAG):
                build(g, g)
            with dve.Fori(0, ITER - 1) as i:
                turns(i, RING + LAG)
            turns(ITER - 1, RING)
            dve.wait_ge(acc_done, BANKS + (k + 1) * (NG + 1))
            dve.sem_inc(agg_ready, 1)

        def dve_sum_general(dve, k):
            for n, (kk, relations, before) in enumerate(ROUNDS):
                if kk != k:
                    continue
                rels_before = sum(x[1] for x in ROUNDS[:n])
                link(dve.memset(rel[:, :], 0.0))

                def tile(r, t):
                    c = bass.ds(t, 1)
                    dve.wait_ge(g_seg, r * NT + t + (before + 1))
                    ins = dve.tensor_tensor(g_key[:, :], local[:, c].broadcast_to([P, NC]), starts[:, :],
                                            ALU.subtract)
                    coef = None
                    if n == 0:
                        ins = dve.tensor_scalar(g_types[:, :], iota[:, 0:R2], type10[:, c], None, ALU.is_equal)
                    elif relations == 1:
                        coef = weight[:, c] if WEIGHTED[k] else None
                    else:
                        types = key if k == 0 else type10
                        coef = g_coef[:, :]
                        if WEIGHTED[k]:
                            ins = dve.tensor_scalar(coef, types[:, c], rel[:, :], weight[:, c],
                                                    ALU.is_equal, ALU.mult)
                        else:
                            ins = dve.tensor_scalar(coef, types[:, c], rel[:, :], None, ALU.is_equal)
                    ins.then_inc(g_step, 1)
                    dve.wait_ge(g_step, r * NT + t + (before + 1))
                    for q in range(NC):
                        if coef is None:
                            last = dve.tensor_scalar(wide[:, q, :], iota[:, :], g_key[:, q:q + 1], None,
                                                     ALU.is_equal)
                        else:
                            last = dve.tensor_scalar(wide[:, q, :], iota[:, :], g_key[:, q:q + 1], coef,
                                                     ALU.is_equal, ALU.mult)
                    last.then_inc(g_oh, 1)

                with dve.Fori(0, relations) as r:
                    with dve.Fori(0, NT) as t:
                        tile(r, t)
                    dve.wait_ge(g_seg, r * NT + (before + NT + 1))
                    for q in range(NC):
                        w = min(CHUNK, N - q * CHUNK)
                        if n == 0:
                            dve.tensor_copy(counts[:, q * CHUNK:q * CHUNK + w], bank[q][0:R2, 0:w])
                        else:
                            dve.tensor_copy(agg[:, bass.ds(r * NA + q * CHUNK, w)], bank[q][:, 0:w])
                    dve.tensor_scalar(rel[:, :], rel[:, :], 1.0, None, ALU.add).then_inc(g_rel, 1)
                    dve.wait_ge(g_rel, r + (rels_before + 1))
            dve.sem_inc(agg_ready, 1)

        def dve_combine(dve, k, b, n_norms):
            m, o = rows(b), b % 2
            dve.wait_ge(tr_done, k * NB + b + 1)
            xb, h = x[0:m, b, :], hb[0:m, b, :]
            if k == 0:
                dve.tensor_tensor(xb, xb, bank[o][0:m, 0:F], ALU.add).then_inc(tr_used, 1)
            elif k == 1:
                dve.scalar_tensor_tensor(xb, bank[o][0:m, 0:F], adeg[0:m, b:b + 1], xb,
                                         ALU.mult, ALU.add).then_inc(tr_used, 1)
            elif k in (2, 3):
                acc = h if k == 2 else xb
                for r in range(R2):
                    ps = bank[3 * o + r // 4][0:m, (r % 4) * F:(r % 4 + 1) * F]
                    ins = dve.scalar_tensor_tensor(acc, ps, inv10[0:m, b, r:r + 1], acc, ALU.mult, ALU.add)
                    if r < R2 - 1:
                        link(ins)
                ins.then_inc(tr_used, 1)
            else:
                dve.scalar_tensor_tensor(h, bank[o][0:m, 0:F], invdeg[0:m, b:b + 1], h,
                                         ALU.mult, ALU.add).then_inc(tr_used, 1)
                dve.wait_ge(tr_used, k * NB + b + 1)
                mark(dve.tensor_tensor_reduce(out=hT[0:m, b % 2, :], in0=h, in1=h, scale=1.0, scalar=0.0,
                                              op0=ALU.mult, op1=ALU.add, accum_out=shift[0:m, b:b + 1]))
                if b % BATCH < BATCH - 1:
                    return
                batch = b // BATCH
                b0 = batch * BATCH
                meet()
                dve.sem_inc(stats_ready, 1)
                dve.wait_ge(std_ready, n_norms * NBATCH + batch + 1)
                rn = rstd[:, b0:b0 + BATCH]
                link(dve.tensor_scalar(rn, rn, NORM_EPS, None, ALU.max))
                link(dve.reciprocal(rn, rn))
                for c in range(b0, b0 + BATCH):
                    mc = rows(c)
                    last = dve.scalar_tensor_tensor(x[0:mc, c, :], hb[0:mc, c, :], rstd[0:mc, c:c + 1],
                                                    x[0:mc, c, :], ALU.mult, ALU.add)
                last.then_inc(x_ready, 1)

        def dve_degrees(dve):
            dve.wait_ge(cnt_T, 1)
            parts = [(P, 0, NFULL), (NREST, NFULL, NB)]
            for m, b0, b1 in parts:
                ps = bank[7][0:m, b0 * R2:b1 * R2].rearrange("p (b r) -> p b r", r=R2)
                mark(dve.tensor_reduce(invdeg[0:m, b0:b1], ps, X, ALU.add))
                mark(dve.tensor_scalar(inv10[0:m, b0:b1, :], ps, 1.0, None, ALU.max))
            meet()
            link(dve.tensor_scalar(invdeg[:, :], invdeg[:, :], 1.0, None, ALU.max))
            mark(dve.reciprocal(inv10[:, :, :], inv10[:, :, :]))
            link(dve.reciprocal(invdeg[:, :], invdeg[:, :]))
            link(dve.tensor_scalar(adeg[:, :], invdeg[:, :], alpha[:, :], None, ALU.mult))

        def dve_skip(dve, k):
            dve.wait_ge(wload[k], 16 * 2)
            dve.wait_ge(h_ready, (k + 1) * NBATCH)
            link(dve.tensor_scalar(root[:, :], bias[:, :], alpha[:, :], None, ALU.mult))
            for m, b0, b1 in [(P, 0, NFULL), (NREST, NFULL, NB)]:
                mark(dve.tensor_tensor(x[0:m, b0:b1, :], x[0:m, b0:b1, :], hb[0:m, b0:b1, :], ALU.add))
            meet()
            for m, b0, b1 in [(P, 0, NFULL), (NREST, NFULL, NB)]:
                mark(dve.tensor_tensor(x[0:m, b0:b1, :], x[0:m, b0:b1, :],
                                       root[0:m, :].unsqueeze(1).broadcast_to([m, b1 - b0, F]), ALU.add))
            meet()

        def dve_path(dve, fast):
            norms = roots = 0
            for k in range(PASSES):
                for batch in range(NBATCH):
                    if k:
                        for b in range(batch * BATCH, (batch + 1) * BATCH):
                            dve_combine(dve, k - 1, b, norms)
                        dve.wait_ge(tr_used, (k - 1) * NB + (batch + 1) * BATCH)
                    if k != 3:
                        dve_stats(dve, norms, batch)
                norms += k != 3
                if k == 1:
                    dve_degrees(dve)
                    dve_skip(dve, k)
                if k >= 2:
                    dve_root(dve, roots, k)
                    roots += 1
                if fast:
                    if k == 2:
                        link(dve.scalar_tensor_tensor(key[:, :], type10[:, :], float(WIN), local[:, :],
                                                      ALU.mult, ALU.add))
                    dve_sum_groups(dve, k)
                else:
                    dve_sum_general(dve, k)
            for b in range(NB):
                dve_combine(dve, PASSES - 1, b, norms)

        @block.vector
        def _(dve):
            for t, v in ((mv, 0.0), (eps, LN_EPS), (ones, 1.0), (shift, 0.0), (invdeg, 1.0), (inv10, 1.0)):
                mark(dve.memset(t[:], v))
            for q in range(NC):
                mark(dve.memset(starts[:, q:q + 1], float(q * CHUNK)))
            dve.wait_ge(loaded, 16 * LOADS)
            mark(dve.tensor_copy(dst_f, dst_i))
            mark(dve.tensor_copy(base_f, base_i))
            link(dve.tensor_copy(type8_f, type8_i))
            link(dve.tensor_tensor(local[:, :].rearrange("p (g t) -> p g t", t=GT),
                                   dst_f.rearrange("p (g t) -> p g t", t=GT),
                                   base_f.unsqueeze(2).broadcast_to([P, NG, GT]), ALU.subtract))
            link(dve.tensor_scalar(top, local[:, :], 0.0, None, ALU.is_ge))
            link(dve.scalar_tensor_tensor(top, local[:, :], float(WIN), top, ALU.is_lt, ALU.mult))
            link(dve.scalar_tensor_tensor(top, dst_f, float(PAD_DST), top, ALU.is_ge, ALU.max))
            dve.tensor_reduce(good[:, :], top, X, ALU.add).then_inc(good_ready, 1)
            dve.wait_ge(flag_sum, 1)
            dve.tensor_scalar(flag[:, :], bank[7][0:1, 0:1], P * NT - 0.5, None, ALU.is_ge).then_inc(flag_ok, 1)
            link(dve.tensor_reduce(top, logits, X, ALU.max))
            link(dve.tensor_tensor(firsts, logits, top.unsqueeze(2).broadcast_to([P, NT, R2]), ALU.is_equal))
            dve.wait_ge(pool_prep, 3)
            link(dve.tensor_scalar(down[:, :], iota[:, 0:R2], -1.0, float(R2), ALU.mult, ALU.add))
            link(dve.tensor_tensor(firsts, firsts, down[:, :].unsqueeze(1).broadcast_to([P, NT, R2]), ALU.mult))
            link(dve.tensor_reduce(type10[:, :], firsts, X, ALU.max))
            link(dve.tensor_scalar(type10[:, :], type10[:, :], -1.0, float(R2), ALU.mult, ALU.add))
            for c in range(NBASES):
                for r in range(R0):
                    s = comp[:, r * NBASES + c:r * NBASES + c + 1]
                    if c == 0:
                        mark(dve.tensor_scalar(wts[:, r, :], basis[:, c, :], s, None, ALU.mult))
                    else:
                        mark(dve.scalar_tensor_tensor(wts[:, r, :], basis[:, c, :], s, wts[:, r, :],
                                                      ALU.mult, ALU.add))
                meet()
            dve.wait_ge(flag_ok, 1)
            fast = dve.value_load(flag[0:1, 0:1], min_val=0, max_val=1)
            steps = step[0]
            with dve.If(fast > 0):
                link(dve.scalar_tensor_tensor(key[:, :], type8_f, float(WIN), local[:, :],
                                              ALU.mult, ALU.add))
                dve_path(dve, True)
            with dve.Else():
                step[0] = steps
                mark(dve.tensor_copy(key[:, :], type8_f))
                link(dve.tensor_copy(local[:, :], dst_f))
                dve_path(dve, False)
            dve.nop()


def _layout(inputs):
    import numpy as np
    a = {n: np.asarray(v) for n, v in inputs.items()}
    E = a["src"].shape[0]
    group = GT * P
    NG = -(-E // (group * RING)) * RING
    NT = NG * GT

    def tiled(v, fill):
        full = np.full((NT * P,) + v.shape[1:], fill, v.dtype)
        full[:E] = v
        return np.ascontiguousarray(np.moveaxis(full.reshape((NT, P) + v.shape[1:]), 0, 1))

    firsts = a["dst"][::group]
    base = np.full(NG, a["x"].shape[0] - 1, firsts.dtype)
    base[:len(firsts)] = firsts
    return {
        "x": a["x"],
        "src": tiled(a["src"], 0),
        "dst": tiled(a["dst"], PAD_DST),
        "base": base,
        "type8": tiled(a["edge_type_8"], 0),
        "logits": tiled(a["edge_attr_42"][:, EMB:-EMB], 0),
        "weight": tiled(a["edge_weight"], 0),
        "comp": a["L0_gnn_w_comp"].reshape(-1),
        "bases": a["L0_gnn_bases"],
        "w1t": np.ascontiguousarray(a["L1_gnn_W"].T),
        "b1": a["L1_gnn_b"],
        "alpha": a["L1_gnn_alpha"].reshape(1),
        "wrel_a": a["L2_gnn_w_rel1"].reshape(-1, F),
        "root_a": a["L2_gnn_root1"],
        "bias_a": a["L2_gnn_b1"],
        "wrel_b": a["L2_gnn_w_rel2"].reshape(-1, F),
        "root_b": a["L2_gnn_root2"],
        "bias_b": a["L2_gnn_b2"],
        "w3rel": np.ascontiguousarray(a["L3_gnn_W_rel"].T),
        "b3": a["L3_gnn_b_rel"],
        "w3root": np.ascontiguousarray(a["L3_gnn_W_root"].T),
    }


def kernel(**inputs):
    import concourse.bacc as _bacc
    from concourse import mybir as _mybir
    from concourse.bass_utils import run_bass_kernel_spmd as _run

    nc = _bacc.Bacc("TRN2", target_bir_lowering=False, num_devices=1)
    arrays, args = {}, []
    for name, a in _layout(inputs).items():
        arrays[f"in_{name}"] = a
        args.append(nc.dram_tensor(f"in_{name}", a.shape, _mybir.dt.from_np(a.dtype), kind="ExternalInput").ap())
    shape = inputs["x"].shape
    args.append(nc.dram_tensor("out_0", shape, _mybir.dt.float32, kind="ExternalOutput").ap())
    graph_layers(nc, *args)
    r = _run(nc, [arrays], core_ids=[0])
    return r.results[0]["out_0"]
```

```python
import concourse.bass as bass
from concourse import mybir
from contextlib import ExitStack


F32 = mybir.dt.float32
BF16 = mybir.dt.bfloat16
F16 = mybir.dt.float16
I32 = mybir.dt.int32
ALU = mybir.AluOpType
ACT = mybir.ActivationFunctionType
X = mybir.AxisListType.X

P = 128
F = 128
WIN = 14
GT = 2
RING = 8
OHRING = 4
BANKS = 2
HALF = 4
PAIR = 2
LAG = 3
BODY = 16
HEAD = 24
SLOTS = 4
RW = SLOTS * P + WIN
CAP = 96
EDGES_PER_NODE = 32
STEP = GT * P // EDGES_PER_NODE
LATE, EARLY = 32, 128
CHUNK = 512
PIECE = 5
R0 = 8
NBASES = 4
R2 = 10
EMB = 16
SEM_TOP = 65535
PAD_DST = 4096
LN_EPS = 1e-5
NORM_EPS = 1e-12
AT_ONCE = 4
PE_LOADS = {0: 4, 2: 8}
PASSES = 5
FIN = 16
TAKEN_BY_ACT = [3]
EXTRA = 8
RELS = [R0, 1, R2, R2, 1]
WEIGHTED = [True, True, False, False, False]
GATHER = {0: 0, 2: 1, 3: 2}
DENSE = {1: 0, 4: 1}
ROOTS = {2: 0, 3: 1, 4: 2}
COUNTS = [0]
NORMS = {0: 0, 1: 1, 3: 2, 4: 3}
BUILDS = {0: 0, 2: 1}


def graph_layers(nc, x_in, src_in, dst_in, base_in, type8_in, logit_in, w_in, comp_in, bases_in,
                 w1t_in, b1_in, alpha_in, wrel_a_in, root_a_in, bias_a_in, wrel_b_in, root_b_in, bias_b_in,
                 w3rel_in, b3_in, w3root_in, out):
    N = x_in.shape[0]
    NT = src_in.shape[1]
    NG = NT // GT
    ITER = NG // RING
    NB = -(-N // P)
    NFULL = N // P
    NREST = N - NFULL * P
    NC = -(-N // CHUNK)
    PIECES = NB // PIECE
    NFC = NC - 1
    ND = N + CAP
    EARLY_CHUNK = STEP * RING * 2 * (NB - 2 - PIECES) - LATE >= CHUNK
    BATCH = 5
    NBATCH = NB // BATCH
    assert NB % BATCH == 0 and NREST > 0 and PAD_DST >= NC * CHUNK and NFULL == 4 * NFC
    assert NG == HEAD + BODY * (NB - 2) and STEP * BODY == P

    assert NB % PIECE == 0 and PAD_DST - N >= NB * WIN

    def rows(b):
        return NREST if isinstance(b, int) and b == NFULL else P

    tables = [nc.dram_tensor(f"node_table{i}", [N, F], F32).ap() for i in range(2)]
    adj = [nc.dram_tensor("adjacency_weights", [P, NB, ND], F32).ap(),
           nc.dram_tensor("adjacency_counts", [P, NB, ND], BF16).ap()]

    ctx = ExitStack()
    with ctx:
        def sb(name, shape, dt=F32):
            return ctx.enter_context(nc.sbuf_tensor(name, shape, dt))

        def sem(name):
            return ctx.enter_context(nc.semaphore(name))

        x = sb("x", [P, NB, F])
        hb = sb("hb", [P, NB, F])
        src = sb("src", [P, NT + RING * GT], I32)
        weight = sb("weight", [P, NT + EXTRA])
        local = sb("local", [P, NT + EXTRA])
        key = sb("key", [P, NT + EXTRA])
        type10 = sb("type10", [P, NT + EXTRA])
        stage = sb("stage", [P, RING // PAIR, PAIR * GT], I32)
        work = sb("work", [P, NB * F + RING * GT * F + OHRING * GT * R2 * WIN])
        h2 = work[:, 0:NB * F].rearrange("p (b f) -> p b f", f=F)
        msg = work[:, NB * F:NB * F + RING * GT * F].rearrange("p (s f) -> p s f", f=F)
        oh = work[:, NB * F + RING * GT * F:].rearrange("p (s c) -> p s c", c=R2 * WIN)
        g_msg = work[:, 0:F]
        wide = work[:, F:F + NC * CHUNK].rearrange("p (c n) -> p c n", n=CHUNK)
        t_oh = sb("t_oh", [P, 2, HALF * GT, R2], BF16)
        n_oh = sb("n_oh", [P, 2, HALF * GT, WIN], BF16)
        wts = sb("wts", [P, R2, F])
        root = sb("root", [P, F])
        bias = sb("bias", [P, F])
        hT = sb("hT", [P, 2, P])
        ident = sb("ident", [P, P])
        ident_h = sb("ident_h", [P, P], BF16)
        iota = sb("iota", [P, CHUNK])
        iota_h = sb("iota_h", [P, NB * WIN], F16)
        comp = sb("comp", [P, R0 * NBASES])
        inv10 = sb("inv10", [P, NB, R2])
        invdeg = sb("invdeg", [P, NB])
        adeg = sb("adeg", [P, NB])
        first_slot = sb("first_slot", [P, NB])
        other_slot = sb("other_slot", [P, NB])
        mv = sb("mv", [P, NB, 2])
        rstd = sb("rstd", [P, NB])
        shift = sb("shift", [P, NB])
        stats = sb("stats", [P, BATCH, 6])
        cols = sb("cols", [P, 10])
        alpha, eps, ones, zero, rel, g_coef, f_std, f_inv, f_shift, f_sq = (cols[:, i:i + 1] for i in range(10))
        f_mv = sb("f_mv", [P, 2])
        g_types = sb("g_types", [P, R2])
        g_key = sb("g_key", [P, NC])
        starts = sb("starts", [P, NC])
        down = sb("down", [P, R2], BF16)
        checks = sb("checks", [P, 4])
        good = sb("good", [P, 1])
        flag = sb("flag", [1, 1], I32)
        base_row = sb("base_row", [1, NG + 1], I32)
        ring_row = sb("ring_row", [1, NG], I32)
        place_row = sb("place_row", [1, NG], I32)
        carry_row = sb("carry_row", [1, NG], I32)
        fast_cols = (R2 * RW + NB * 2 * CAP + 2 * (NT + EXTRA) + OHRING * GT * (NB * WIN + P) + GT * P
                     + (R2 + 2) * P + CHUNK + PIECES * PIECE * CHUNK)
        prep_cols = R2 * RW + NB * 2 * CAP + 2 * (NT + EXTRA) + NT * (R2 + 7 + R2 // 2) + 4 * NG + 2
        AGG = max(R2 * N, fast_cols, prep_cols)
        agg = sb("agg", [P, AGG])
        bank = [ctx.enter_context(nc.psum_tensor(f"bank{i}", [P, CHUNK], F32)) for i in range(8)]

        col = [0]

        def carve(n, dt=F32):
            a = agg[:, col[0]:col[0] + n]
            col[0] += n
            assert col[0] <= AGG
            return a if dt == F32 else a.bitcast(dt)

        ring = carve(R2 * RW).rearrange("p (r n) -> p r n", n=RW)
        abuf_w = carve(NB * 2 * CAP)
        abufs = [abuf_w.rearrange("p (b s n) -> p b s n", s=2, n=CAP),
                 abuf_w[:, 0:NB * CAP].bitcast(BF16).rearrange("p (b s n) -> p b s n", s=2, n=CAP)]
        neglo = carve(NT + EXTRA)
        akey = carve(NT + EXTRA)
        col_prep = col[0]
        a_oh_w = carve(OHRING * GT * NB * WIN)
        a_ohs = [a_oh_w.rearrange("p (s n) -> p s n", n=NB * WIN),
                 a_oh_w.bitcast(BF16)[:, 0:OHRING * GT * NB * WIN].rearrange("p (s n) -> p s n", n=NB * WIN)]
        lo_oh_w = carve(OHRING * GT * P)
        lo_ohs = [lo_oh_w.rearrange("p (s n) -> p s n", n=P),
                  lo_oh_w.bitcast(BF16)[:, 0:OHRING * GT * P].rearrange("p (s n) -> p s n", n=P)]
        dist = carve(GT * P).rearrange("p (s n) -> p s n", n=P)
        S = carve(R2 * P).rearrange("p (r n) -> p r n", n=P)
        acc = carve(P)
        hstat = carve(P)
        aT = carve(CHUNK)
        piece_w = carve(PIECES * PIECE * CHUNK)
        pieces = [piece_w.rearrange("p (s b n) -> p s b n", s=PIECES, n=CHUNK),
                  piece_w[:, 0:PIECES * PIECE * CHUNK // 2].bitcast(BF16).rearrange(
                      "p (s b n) -> p s b n", s=PIECES, n=CHUNK)]
        splits = piece_w[:, PIECES * PIECE * CHUNK // 2:PIECES * PIECE * CHUNK // 2 + 3 * NB * F // 2].bitcast(
            BF16).rearrange("p (s b f) -> p s b f", s=3, f=F)

        col[0] = col_prep
        logits = carve(NT * R2).rearrange("p (t r) -> p t r", r=R2)
        dst_i = carve(NT, I32)
        type8_i = carve(NT, I32)
        base_i = carve(NG + 1, I32)
        dst_f = carve(NT)
        type8_f = carve(NT)
        hi_f = carve(NT)
        low_i = carve(NT, I32)
        base_f = carve(NG + 1)
        off_f = carve(NG)
        okb = carve(NG)
        top = carve(NT)
        basis = work[:, 0:NBASES * F].rearrange("p (b f) -> p b f", f=F)
        eq = carve(NT * R2 // 2).bitcast(BF16).rearrange("p (t r) -> p t r", r=R2)
        counts = agg[0:R2, R0 * N:(R0 + 1) * N]

        def by_relation(n):
            return agg[:, 0:n * N].rearrange("p (r n) -> p r n", n=N)

        x_loaded = sem("x_loaded")
        loaded = sem("loaded")
        wload = [sem(f"wload{k}") for k in range(PASSES)]
        prep = sem("prep")
        pool_prep = sem("pool_prep")
        fast_ready = sem("fast_ready")
        good_ready = sem("good_ready")
        flag_sum = sem("flag_sum")
        flag_ok = sem("flag_ok")
        stats_ready = sem("stats_ready")
        std_ready = sem("std_ready")
        scale_ready = sem("scale_ready")
        h_ready = sem("h_ready")
        table_ready = sem("table_ready")
        agg_ready = sem("agg_ready")
        tr_done = sem("tr_done")
        tr_used = sem("tr_used")
        rt_T = sem("rt_T")
        rt_c = sem("rt_c")
        rt_mm = sem("rt_mm")
        rt_used = sem("rt_used")
        cnt_T = sem("cnt_T")
        cnt_used = sem("cnt_used")
        x_ready = sem("x_ready")
        out_sem = sem("out_sem")
        idx_ready = sem("idx_ready")
        gathered = [sem(f"gathered{s}") for s in range(RING * GT)]
        oh_ready = sem("oh_ready")
        seg_done = sem("seg_done")
        acc_done = sem("acc_done")
        pool_go = sem("pool_go")
        act_go, dve_go, sp_go = sem("act_go"), sem("dve_go"), sem("sp_go")
        a_ready = sem("a_ready")
        dist_ready = sem("dist_ready")
        lo_ready = sem("lo_ready")
        adj_done = sem("adj_done")
        placed = sem("placed")
        flushed = sem("flushed")
        taken = sem("taken")
        zeroed = sem("zeroed")
        S_ready = sem("S_ready")
        hs_ready = sem("hs_ready")
        hs_T = sem("hs_T")
        hT_ready = sem("hT_ready")
        prod_done = sem("prod_done")
        comb_done = sem("comb_done")
        fin = sem("fin")
        var_ready = sem("var_ready")
        dev_ready = sem("dev_ready")
        affine_ready = sem("affine_ready")
        h_done = sem("h_done")
        stored = sem("stored")
        split_ready = sem("split_ready")
        piece_loaded = [sem(f"piece_loaded{p}") for p in range(PIECES)]
        piece_used = sem("piece_used")
        dense_done = sem("dense_done")
        aT_ready = sem("aT_ready")
        logits_loaded = sem("logits_loaded")
        mixed = sem("mixed")
        x_done = sem("x_done")
        g_idx = sem("g_idx")
        g_step = sem("g_step")
        g_rel = sem("g_rel")
        g_oh = sem("g_oh")
        g_seg = sem("g_seg")

        step = [0]

        def link(ins):
            step[0] += 1
            ins.then_inc(prep, 1)
            nc.vector.wait_ge(prep, step[0])

        def mark(ins):
            step[0] += 1
            ins.then_inc(prep, 1)

        def meet():
            nc.vector.wait_ge(prep, step[0])

        at_most = SEM_TOP // (16 * NT)
        ROUNDS, before = [], 0
        for k, relations in [(0, 1)] + list(enumerate(RELS)):
            for first in range(0, relations, at_most):
                n = min(at_most, relations - first)
                ROUNDS.append((k, first, n, before))
                before += n * NT
        g_gathered = [sem(f"g_gathered{n}") for n in range(len(ROUNDS))]

        def ring_place(b):
            at = (b % SLOTS) * P
            return at if isinstance(b, int) else nc.s_assert_within(at, 0, (SLOTS - 1) * P)

        def block_of(t, b):
            return t[0:rows(b), bass.ds(b, 1), :]

        block = ctx.enter_context(nc.Block())

        TABLE_DMAS = NBATCH + 1

        def store_rows(sp, dram, batch, tile, semaphore):
            b0, b1 = batch * BATCH, min((batch + 1) * BATCH, NFULL)
            sp.dma_start(dram[b0 * P:b1 * P, :].rearrange("(b p) f -> p b f", p=P),
                         tile[:, b0:b1, :]).then_inc(semaphore, 16)
            if batch == NBATCH - 1:
                sp.dma_start(dram[NFULL * P:N, :], tile[0:NREST, NFULL, :]).then_inc(semaphore, 16)

        def load_weights(sp, k):
            w_src, r_src, b_src = [(None, None, None), (w1t_in, None, b1_in),
                                   (wrel_a_in, root_a_in, bias_a_in), (wrel_b_in, root_b_in, bias_b_in),
                                   (w3rel_in, w3root_in, b3_in)][k]
            n = RELS[k]
            sp.dma_start(wts[:, 0:n, :], w_src.rearrange("(r d) f -> d r f", d=F)).then_inc(wload[k], 16)
            if r_src is not None:
                sp.dma_start(root[:, :], r_src).then_inc(wload[k], 16)
            sp.dma_start(bias[:, :], b_src.partition_broadcast(P)).then_inc(wload[k], 16)

        def store_table(sp, k):
            for batch in range(NBATCH):
                sp.wait_ge(h_ready, k * NBATCH + batch + 1)
                store_rows(sp, tables[0], batch, hb, table_ready)

        def sp_general(sp):
            for k in range(1, PASSES):
                store_table(sp, k)
                sp.wait_ge(tr_used, k * NB)
                load_weights(sp, k)
            for batch in range(NBATCH):
                sp.wait_ge(x_ready, batch + 1)
                store_rows(sp, out, batch, x, out_sem)
            sp.wait_ge(out_sem, 16 * TABLE_DMAS)

        def sp_flush_ring(sp, k, r, parity):
            ai = BUILDS[k]
            base = sp.value_load(base_row[0:1, bass.ds(RING * r, 1)], min_val=0, max_val=N - 1)
            sp.wait_ge(placed, RING * r + (BANKS + ai * NG + RING))
            sp.sem_inc(sp_go, 1)
            sp.wait_ge(flushed, 16 * r + 16 * ai * ITER)
            sp.sem_inc(sp_go, 1)
            sp.dma_start(adj[ai][:, :, bass.ds(base, CAP)],
                         abufs[ai][:, :, parity, :]).then_inc(flushed, 16)

        def sp_store_block(sp, k, b):
            m = rows(b)
            sp.wait_ge(h_done, b + (k * NB + 2))
            sp.sem_inc(sp_go, 1)
            sp.dma_start(tables[k - 1][bass.ds(b * P, m), :], block_of(h2, b)[:, 0, :]).then_inc(stored, 16)

        def sp_gather_pass(sp, k):
            for r in range(HEAD // RING):
                sp_flush_ring(sp, k, r, r % 2)

            def body(j):
                sp_flush_ring(sp, k, 2 * j + 3, 1)
                if k == 2:
                    sp_store_block(sp, k, j)
                sp_flush_ring(sp, k, 2 * j + 4, 0)

            early = PIECES if k == 0 and EARLY_CHUNK else 0
            with sp.Fori(0, NB - 2 - early) as j:
                body(j)
            for j in range(NB - 2 - early, NB - 2):
                sp_load_chunk(sp, 1, 0, True, [j - (NB - 2 - early)])
                body(j)
            if k == 2:
                for b in range(NB - 2, NB):
                    sp_store_block(sp, k, b)

        def sp_load_chunk(sp, k, c, first, which=range(PIECES)):
            d = DENSE[k]
            w = CHUNK if not isinstance(c, int) else min(CHUNK, N - c * CHUNK)
            for p in which:
                if not first:
                    sp.wait_ge(piece_used, c * PIECES + ((d * NC - 1) * PIECES + p + 1))
                    sp.sem_inc(sp_go, 1)
                sp.dma_start(pieces[d][:, p, :, 0:w],
                             adj[d][:, p * PIECE:(p + 1) * PIECE, bass.ds(c * CHUNK, w)]
                             ).then_inc(piece_loaded[p], 16)

        def sp_leave_block(sp, k, b):
            if k == 1:
                sp_store_block(sp, k, b)
            else:
                m = rows(b)
                sp.wait_ge(x_done, b + 1)
                sp.sem_inc(sp_go, 1)
                sp.dma_start(out[bass.ds(b * P, m), :], block_of(x, b)[:, 0, :]).then_inc(out_sem, 16)

        def sp_dense_pass(sp, k):
            if NFC > 1:
                sp_load_chunk(sp, k, 1, False)
                with sp.Fori(1, NFC - 1) as c:
                    sp_load_chunk(sp, k, c + 1, False)
                    for i in range(SLOTS):
                        sp_leave_block(sp, k, SLOTS * c + (i - SLOTS))
            sp_load_chunk(sp, k, NFC, False)
            for b in range(SLOTS * max(NFC - 2, 0), NB):
                sp_leave_block(sp, k, b)

        def sp_weights(sp, k):
            sp.wait_ge(prod_done, k * NB + 1)
            sp.wait_ge(comb_done, k * NB + 1)
            load_weights(sp, k)

        def sp_fast(sp):
            sp.wait_ge(fast_ready, 1)
            sp_gather_pass(sp, 0)
            sp.wait_ge(flushed, 16 * ITER)
            if not EARLY_CHUNK:
                sp_load_chunk(sp, 1, 0, True)
            sp_weights(sp, 1)
            sp_dense_pass(sp, 1)
            sp_weights(sp, 2)
            sp_gather_pass(sp, 2)
            sp.wait_ge(flushed, 16 * 2 * ITER)
            sp_load_chunk(sp, 4, 0, True)
            sp_weights(sp, 3)
            sp_weights(sp, 4)
            sp_dense_pass(sp, 4)
            sp.wait_ge(out_sem, 16 * NB)

        @block.sync
        def _(sp):
            sp.dma_start(x[:, 0:NFULL, :], x_in[0:NFULL * P, :].rearrange("(b p) f -> p b f", p=P)
                         ).then_inc(x_loaded, 16)
            sp.dma_start(x[0:NREST, NFULL, :], x_in[NFULL * P:N, :]).then_inc(x_loaded, 16)
            sp.dma_start(dst_i, dst_in).then_inc(loaded, 16)
            sp.dma_start(base_i, base_in.partition_broadcast(P)).then_inc(loaded, 16)
            sp.dma_start(base_row[:, :], base_in.rearrange("(o g) -> o g", o=1)).then_inc(loaded, 16)
            sp.dma_start(type8_i, type8_in).then_inc(loaded, 16)
            sp.dma_start(weight[:, 0:NT], w_in).then_inc(loaded, 16)
            sp.dma_start(src[:, 0:NT], src_in).then_inc(loaded, 16)
            sp.dma_start(src[:, NT:], src_in[:, 0:RING * GT]).then_inc(loaded, 16)
            sp.dma_start(logits, logit_in).then_inc(logits_loaded, 16)
            sp.dma_start(basis, bases_in.rearrange("b d f -> d b f")).then_inc(loaded, 16)
            sp.dma_start(comp[:, :], comp_in.partition_broadcast(P)).then_inc(loaded, 16)
            sp.dma_start(alpha, alpha_in.partition_broadcast(P)).then_inc(loaded, 16)
            store_table(sp, 0)
            sp.wait_ge(flag_ok, 1)
            fast = sp.value_load(flag[0:1, 0:1], min_val=0, max_val=1)
            with sp.If(fast > 0):
                sp_fast(sp)
            with sp.Else():
                sp_general(sp)
            sp.nop()

        LOADS = 10

        def gather(pool, dst, index, table=tables[0]):
            return pool.indirect_dma_start(dst, None, table, bass.IndirectOffsetOnAxis(ap=index, axis=0))

        def pool_fast(pool):
            for k, gi in GATHER.items():
                if k == 0:
                    pool.wait_ge(table_ready, 16 * TABLE_DMAS)
                else:
                    if k == 2:
                        pool.wait_ge(flushed, 16 * ITER)
                        pool.memset(abuf_w[:, 0:NB * CAP], 0.0).then_inc(pool_prep, 1)
                    pool.wait_ge(stored, 16 * NB * gi)
                with pool.Fori(0, ITER) as i:
                    for u in range(RING):
                        if u % PAIR == 0:
                            pool.wait_ge(idx_ready, (RING // PAIR) * i + (gi * NG // PAIR + u // PAIR + 1))
                            pool.sem_inc(pool_go, 1)
                        for j in range(GT):
                            s = u * GT + j
                            gather(pool, msg[:, s, :],
                                   stage[:, u // PAIR, s % (PAIR * GT):s % (PAIR * GT) + 1],
                                   tables[1 if k == 3 else 0]).then_inc(gathered[s], 16)

        def pool_general(pool):
            for n, (k, _, relations, before) in enumerate(ROUNDS):
                if n != 1:
                    pool.wait_ge(table_ready, 16 * TABLE_DMAS * (k + 1))
                    pool.sem_inc(pool_go, 1)
                with pool.Fori(0, relations * NT) as t:
                    pool.wait_ge(g_idx, t + (before + 1))
                    pool.sem_inc(pool_go, 1)
                    gather(pool, g_msg, stage[:, 0, 0:1]).then_inc(g_gathered[n], 16)

        @block.gpsimd
        def _(pool):
            pool.iota(iota[:, :], [[1, CHUNK]], base=0, channel_multiplier=0,
                      allow_small_or_imprecise_dtypes=True).then_inc(pool_prep, 1)
            pool.memset(ident[:, :], 0.0).then_inc(pool_prep, 1)
            pool.wait_ge(pool_prep, 2)
            pool.affine_select(out=ident[:, :], in_=ident[:, :], compare_op=ALU.not_equal, fill=1.0,
                               base=0, pattern=[[-1, P]], channel_multiplier=1).then_inc(pool_prep, 1)
            pool.iota(iota_h[:, :], [[1, NB * WIN]], base=0, channel_multiplier=0,
                      allow_small_or_imprecise_dtypes=True).then_inc(pool_prep, 1)
            pool.memset(first_slot[:, :], 0.0).then_inc(pool_prep, 1)
            pool.memset(other_slot[:, :], 1.0).then_inc(pool_prep, 1)
            pool.wait_ge(pool_prep, 6)
            pool.tensor_copy(ident_h[:, :], ident[:, :]).then_inc(pool_prep, 1)
            for b in range(0, NB, SLOTS):
                pool.memset(first_slot[:, b:b + 1], 1.0).then_inc(pool_prep, 1)
                pool.memset(other_slot[:, b:b + 1], 0.0).then_inc(pool_prep, 1)
            pool.memset(agg[:, 0:R2 * RW + NB * 2 * CAP], 0.0).then_inc(pool_prep, 1)
            pool.wait_ge(flag_ok, 1)
            fast = pool.value_load(flag[0:1, 0:1], min_val=0, max_val=1)
            with pool.If(fast > 0):
                pool_fast(pool)
            with pool.Else():
                pool_general(pool)
            pool.nop()

        POOL_PREP = 8 + 2 * -(-NB // SLOTS)

        def take(engine, k, b):
            n, q = RELS[k] + (k in COUNTS), GATHER[k] * NB
            slot = ring[:, 0:n, bass.ds(ring_place(b), P)]
            groups = min(BODY * b + HEAD, NG) if isinstance(b, int) else BODY * b + HEAD
            if k in TAKEN_BY_ACT:
                go, copy = act_go, lambda to, what: nc.scalar.activation(to, what, ACT.Copy)
            else:
                go, copy = dve_go, nc.vector.tensor_copy
            engine.wait_ge(acc_done, groups + (GATHER[k] * NG + BANKS))
            engine.wait_ge(prod_done, b + (k * NB + 1))
            engine.sem_inc(go, 1)
            copy(S[:, 0:n, :], slot).then_inc(taken, 1)
            engine.wait_ge(taken, b + (q + 1))
            engine.sem_inc(go, 1)
            copy(slot, zero.unsqueeze(2).broadcast_to([P, n, P])).then_inc(zeroed, 1)

        def act_normalise(act, n, k):
            for batch in range(NBATCH):
                b0 = batch * BATCH
                act.wait_ge(stats_ready, n * NBATCH + batch + 1)
                act.activation(rstd[:, b0:b0 + BATCH], mv[:, b0:b0 + BATCH, 1], ACT.Sqrt,
                               bias=eps[:, :]).then_inc(std_ready, 1)
                act.wait_ge(scale_ready, n * NBATCH + batch + 1)
                if k:
                    act.wait_ge(table_ready, 16 * TABLE_DMAS * k)
                for b in range(b0, b0 + BATCH):
                    m = rows(b)
                    last = act.activation(hb[0:m, b, :], x[0:m, b, :], ACT.Relu,
                                          bias=shift[0:m, b:b + 1], scale=rstd[0:m, b:b + 1])
                last.then_inc(h_ready, 1)

        def act_rectify(act, k):
            for batch in range(NBATCH):
                for b in range(batch * BATCH, (batch + 1) * BATCH):
                    m = rows(b)
                    act.wait_ge(tr_used, (k - 1) * NB + b + 1)
                    last = act.activation(hb[0:m, b, :], hb[0:m, b, :], ACT.Relu)
                last.then_inc(h_ready, 1)

        def act_root(act, n):
            for b in range(NB):
                m = rows(b)
                act.wait_ge(rt_T, n * NB + b + 1)
                act.activation(hT[:, b % 2, 0:m], bank[4 + b % 2][:, 0:m], ACT.Copy).then_inc(rt_c, 1)

        def loads(row, g, n, engine, top):
            _, values = nc.values_load_multi_w_load_instructions(
                row[0:1, bass.ds(g, n)], engines=(engine,), min_val=0, max_val=top)
            return values

        def act_build(act, k, g, u):
            ai = BUILDS[k]
            act.wait_ge(lo_ready, g + ai * (NG + LAG))
            act.sem_inc(act_go, 1)
            for j in range(GT):
                act.activation(dist[:, j, :], iota[:, 0:P], ACT.Abs,
                               bias=neglo[:, bass.ds(GT * g + j, 1)]).then_inc(dist_ready, 1)
            act.wait_ge(dist_ready, GT * g + (GT * ai * (NG + LAG) + GT))
            act.wait_ge(adj_done, g + (ai * NG + 1))
            s = (u % OHRING) * GT
            act.activation(lo_ohs[ai][:, s:s + GT, :], dist[:, :, :], ACT.Relu, bias=ones,
                           scale=-1.0).then_inc(lo_ready, 1)

        def act_place(act, k, g, u, parity, place):
            ai = BUILDS[k]
            act.wait_ge(adj_done, g + (OHRING + ai * NG + 1))
            act.sem_inc(act_go, 1)
            act.activation(abufs[ai][:, :, parity, bass.ds(place, WIN)],
                           bank[2 + u % BANKS][:, 0:NB * WIN].rearrange("p (b n) -> p b n", n=WIN),
                           ACT.Copy).then_inc(placed, 1)

        def act_stage_pair(act, k, g, pair):
            act.wait_ge(seg_done, g + (GATHER[k] * NG + RING + 1))
            act.sem_inc(act_go, 1)
            act.activation(stage[:, pair, :], src[:, bass.ds(GT * g + GT * (RING + 1 - PAIR), PAIR * GT)],
                           ACT.Copy).then_inc(idx_ready, 1)

        def act_copy_nodes(act, k, b):
            m, q = rows(b), ROOTS[k] * NB
            act.wait_ge(hs_T, b + (q + 1))
            act.sem_inc(act_go, 1)
            act.activation(hstat[0:m, :], block_of(h2, b)[:, 0, :], ACT.Copy).then_inc(hs_ready, 1)

        def act_copy_transposed(act, k, b, buf=0):
            m, q = rows(b), ROOTS[k] * NB
            act.wait_ge(hs_T, b + (q + 2))
            act.wait_ge(prod_done, b + (k * NB + (k != 4)))
            act.activation(hT[:, buf, 0:m], bank[4][:, 0:m], ACT.Copy).then_inc(hT_ready, 1)

        def act_deviation(act, k, b):
            m, q = rows(b), NORMS[k] * NB
            act.wait_ge(var_ready, b + (q + 1))
            if k == 4:
                act.activation(f_std[0:m, :], f_sq[0:m, :], ACT.Sqrt).then_inc(dev_ready, 1)
            else:
                act.activation(f_std[0:m, :], f_mv[0:m, 1:2], ACT.Sqrt, bias=eps[0:m, :]).then_inc(dev_ready, 1)

        def act_nodes(act, k, b):
            m = rows(b)
            h = block_of(hb if k == 0 else h2, b)[:, 0, :]
            if k == 2:
                act.wait_ge(comb_done, b + (k * NB + 2))
                act.sem_inc(act_go, 1)
                act.activation(h, acc[0:m, :], ACT.Relu).then_inc(h_done, 1)
            else:
                act.wait_ge(affine_ready, b + (NORMS[k] * NB + 1))
                act.sem_inc(act_go, 1)
                act.activation(h, block_of(x, b)[:, 0, :], ACT.Relu, bias=f_shift[0:m, :],
                               scale=f_inv[0:m, :]).then_inc(h_done, 1)

        def act_gather_pass(act, k):
            builds = k in BUILDS
            if builds and k:
                act.wait_ge(pool_prep, POOL_PREP + 1)
            if builds:
                for g in range(LAG):
                    act_build(act, k, g, g)
            if k >= 2:
                act.wait_ge(stored, 16 * NB * (k - 1))

            def finish(b, u):
                if u == 2 and k in TAKEN_BY_ACT:
                    take(act, k, b)
                if u == 0 and k in ROOTS:
                    act_copy_nodes(act, k, b)
                if u == 1 and k in ROOTS:
                    act_copy_transposed(act, k, b)
                if u == 8 and k in NORMS:
                    act_deviation(act, k, b)
                if u == 13:
                    act_nodes(act, k, b)

            def ring_turns(g, parity, flushes, places, b=None, first_turn=0):
                for u in range(RING):
                    if b is not None:
                        finish(b, first_turn + u)
                    if builds:
                        act_build(act, k, g + u + LAG, u + LAG)
                        if u == 0 and flushes is not None:
                            act.wait_ge(flushed, flushes)
                        act_place(act, k, g + u, u, parity, places[u])
                    if u % PAIR == PAIR - 1:
                        act_stage_pair(act, k, g + u, u // PAIR)

            def load(g, n):
                return loads(place_row, g, n, mybir.EngineType.Activation, CAP - WIN) if builds else [None] * n

            f0 = 16 * BUILDS[k] * ITER if builds else 0
            for r in range(HEAD // RING):
                ring_turns(RING * r, r % 2, f0 + 16 * (r - 1) if r >= 2 else None, load(RING * r, RING))
            with act.Fori(0, NB - 2) as j:
                ring_turns(BODY * j + HEAD, 1, 32 * j + (f0 + 32), load(BODY * j + HEAD, RING), j, 0)
                ring_turns(BODY * j + (HEAD + RING), 0, 32 * j + (f0 + 48),
                           load(BODY * j + (HEAD + RING), RING), j, RING)
            for b in range(NB - 2, NB):
                for u in range(BODY):
                    finish(b, u)

        def act_dense_pass(act, k):
            d = DENSE[k]

            def chunk_copy(c, w):
                act.wait_ge(dense_done, c + (d * NC + 1))
                act.wait_ge(prod_done, SLOTS * c + (k * NB + 1))
                act.activation(aT[:, 0:w], bank[0][:, 0:w], ACT.Copy).then_inc(aT_ready, 1)

            def leave(b):
                act_deviation(act, k, b)
                if k == 1:
                    act_nodes(act, k, b)

            def nodes(b, i):
                if k == 4:
                    act_copy_nodes(act, k, b)
                    act_copy_transposed(act, k, b, i % 2)

            def turn(c, w):
                for i in range(SLOTS):
                    nodes(SLOTS * c + i, i)
                    if i:
                        leave(SLOTS * c + (i - 1))
                chunk_copy(c + 1, w)
                leave(SLOTS * c + (SLOTS - 1))

            chunk_copy(0, CHUNK)
            if NFC > 1:
                with act.Fori(0, NFC - 1) as c:
                    turn(c, CHUNK)
            turn(NFC - 1, NREST)
            nodes(NFULL, NFULL)
            leave(NFULL)

        def act_fast(act):
            act.sem_inc(placed, BANKS)
            act.sem_inc(h_done, 1)
            act.sem_inc(hT_ready, 1)
            for p in range(RING // PAIR):
                act.activation(stage[:, p, :], src[:, p * PAIR * GT:(p + 1) * PAIR * GT],
                               ACT.Copy).then_inc(idx_ready, 1)
            act.wait_ge(fast_ready, 1)
            for k in range(PASSES):
                if k in GATHER:
                    act_gather_pass(act, k)
                else:
                    act_dense_pass(act, k)

        def act_stage_general(act, k):
            for _, _, relations, before in [x for x in ROUNDS if x[0] == k]:
                with act.Fori(0, relations) as r:
                    with act.Fori(0, NT) as t:
                        act.wait_ge(g_seg, r * NT + t + (before + 1))
                        act.activation(stage[:, 0, 0:1], src[:, bass.ds(t, 1)], ACT.Copy).then_inc(g_idx, 1)

        def act_general(act):
            act.wait_ge(mixed, 1)
            norms, roots = 1, 0
            for k in range(PASSES):
                if k == 3:
                    act_rectify(act, k)
                elif k:
                    act_normalise(act, norms, k)
                    norms += 1
                if k >= 2:
                    act_root(act, roots)
                    roots += 1
                act_stage_general(act, k)
            for batch in range(NBATCH):
                b0 = batch * BATCH
                act.wait_ge(stats_ready, norms * NBATCH + batch + 1)
                act.activation(rstd[:, b0:b0 + BATCH], shift[:, b0:b0 + BATCH], ACT.Sqrt).then_inc(std_ready, 1)

        @block.scalar
        def _(act):
            act_normalise(act, 0, 0)
            act.wait_ge(flag_ok, 1)
            fast = act.value_load(flag[0:1, 0:1], min_val=0, max_val=1)
            with act.If(fast > 0):
                act_fast(act)
            with act.Else():
                act_general(act)
            act.nop()

        def pe_root(pe, n, k):
            pe.wait_ge(wload[k], 16 * 3)
            for b in range(NB + 1):
                if b < NB:
                    m = rows(b)
                    pe.wait_ge(h_ready, k * NBATCH + b // BATCH + 1)
                    if n * NB + b >= 2:
                        pe.wait_ge(rt_c, n * NB + b - 1)
                    pe.transpose(bank[4 + b % 2][:, 0:m], hb[0:m, b, :], ident[0:m, 0:m]).then_inc(rt_T, 1)
                if b >= 1:
                    c = b - 1
                    m = rows(c)
                    pe.wait_ge(rt_c, n * NB + c + 1)
                    if n * NB + c >= 2:
                        pe.wait_ge(rt_used, n * NB + c - 1)
                    pe.matmul(bank[6 + c % 2][0:m, 0:F], hT[:, c % 2, 0:m], root[:, :],
                              start=True, stop=True).then_inc(rt_mm, 1)

        def pe_group(pe, k, g, u, ring_no, parity, carry):
            gi, n = GATHER[k], RELS[k] * WIN
            ps = bank[u % BANKS]
            pe.wait_ge(oh_ready, g + (gi * (NG + LAG) + 1))
            pe.wait_ge(acc_done, g + (gi * NG + 1))
            for j in range(GT):
                s = u * GT + j
                pe.wait_ge(gathered[s], ring_no * 16 + 16 * (gi * ITER + 1))
                last = pe.matmul(ps[:, 0:n], msg[:, s, :], oh[:, s % (OHRING * GT), 0:n],
                                 start=(j == 0), stop=(j == GT - 1))
            if k in COUNTS:
                for j in range(GT):
                    s = u * GT + j
                    v = s % (HALF * GT)
                    last = pe.matmul(ps[0:R2, n:n + WIN], t_oh[:, u // HALF, v, :],
                                     n_oh[:, u // HALF, v, :], start=(j == 0), stop=(j == GT - 1))
            last.then_inc(seg_done, 1)
            if k not in BUILDS:
                return
            ai = BUILDS[k]
            pa = bank[2 + u % BANKS][:, 0:NB * WIN]
            pe.wait_ge(a_ready, g + (ai * (NG + LAG) + 1))
            pe.wait_ge(lo_ready, g + (ai * (NG + LAG) + 1))
            pe.wait_ge(placed, g + (ai * NG + 1))
            for j in range(GT):
                s = (u * GT + j) % (OHRING * GT)
                last = pe.matmul(pa, lo_ohs[ai][:, s, :], a_ohs[ai][:, s, :],
                                 start=(j == 0), stop=(j == GT - 1 and carry is None))
            if carry is not None:
                before = parity if u % RING else 1 - parity
                pe.wait_ge(placed, g + (ai * NG + BANKS))
                last = pe.matmul(pa.rearrange("p (b n) -> p b n", n=WIN)[:, :, 0:1],
                                 ident_h[:, :] if ai else ident[:, :],
                                 abufs[ai][:, :, before, bass.ds(carry, 1)], start=False, stop=True)
            last.then_inc(adj_done, 1)

        def pe_turn_nodes(pe, k, b):
            m, q = rows(b), ROOTS[k] * NB
            pe.wait_ge(hs_ready, b + (q + 1))
            pe.wait_ge(hT_ready, b + (q + 1))
            pe.transpose(bank[4][:, 0:m], hstat[0:m, :], ident[0:m, 0:m]).then_inc(hs_T, 1)

        def pe_products(pe, k, b, offset=0, buf=0):
            m = rows(b)
            if k:
                pe.wait_ge(wload[k], 16 * (2 if k == 1 else 3))
            pe.wait_ge(comb_done, b + (k * NB + 1))
            if k in GATHER:
                pe.wait_ge(S_ready, b + (GATHER[k] * NB + 1))
            if k in ROOTS:
                pe.wait_ge(hT_ready, b + (ROOTS[k] * NB + 2))
            if k == 0:
                for r in range(R0):
                    pe.matmul(bank[5][0:m, 0:F], S[:, r, 0:m], wts[:, r, :], start=(r == 0), stop=(r == R0 - 1))
                last = pe.transpose(bank[7][0:m, 0:R2], S[0:R2, R0, 0:m], ident[0:R2, 0:R2])
            elif k in GATHER:
                for r in range(R2):
                    last = pe.matmul(bank[5 + r // 4][0:m, (r % 4) * F:(r % 4 + 1) * F],
                                     S[:, r, 0:m], wts[:, r, :], start=True, stop=True)
                last = pe.matmul(bank[7][0:m, 2 * F:3 * F], hT[:, 0, 0:m], root[:, :], start=True, stop=True)
            else:
                last = pe.matmul(bank[5][0:m, 0:F], aT[:, offset:offset + m], wts[:, 0, :],
                                 start=True, stop=True)
                if k == 4:
                    last = pe.matmul(bank[6][0:m, 0:F], hT[:, buf, 0:m], root[:, :], start=True, stop=True)
            last.then_inc(prod_done, 1)

        def pe_finish(pe, k, b, u):
            if u == 0 and k in ROOTS:
                pe_turn_nodes(pe, k, b)
            if u == 5:
                pe_products(pe, k, b)

        def pe_gather_pass(pe, k):
            def ring_turns(g, ring_no, parity, b=None, first_turn=0):
                carries = [None] * RING
                for u in range(RING):
                    if k in BUILDS and u % PE_LOADS[k] == 0:
                        n = PE_LOADS[k]
                        carries[u:u + n] = loads(carry_row, g + u, n, mybir.EngineType.PE, CAP - 1)
                        if isinstance(g, int) and g + u == 0:
                            carries[0] = None
                    if b is not None:
                        pe_finish(pe, k, b, first_turn + u)
                    pe_group(pe, k, g + u, u, ring_no, parity, carries[u])

            for r in range(HEAD // RING):
                ring_turns(RING * r, r, r % 2)
            with pe.Fori(0, NB - 2) as j:
                ring_turns(BODY * j + HEAD, 2 * j + 3, 1, j, 0)
                ring_turns(BODY * j + (HEAD + RING), 2 * j + 4, 0, j, RING)
            if k + 1 in DENSE and PIECES > 2:
                return
            for b in range(NB - 2, NB):
                for u in range(BODY):
                    pe_finish(pe, k, b, u)

        def pe_dense_pass(pe, k):
            d = DENSE[k]
            before = max(i for kk, i in GATHER.items() if kk < k)
            pe.wait_ge(acc_done, BANKS + (before + 1) * NG)

            def chunk(c, w, last_chunk):
                pe.wait_ge(aT_ready, c + d * NC)
                for p in range(PIECES if last_chunk is None else max(PIECES, SLOTS)):
                    b = None if last_chunk is None or p >= SLOTS else SLOTS * last_chunk + p
                    if b is not None and k == 4:
                        pe_turn_nodes(pe, k, b)
                    late = last_chunk is None and PIECES > 2 and p < 2
                    for u in range(BODY if late else 0):
                        pe_finish(pe, k - 1, NB - 2 + p, u)
                    if p < PIECES:
                        pe.wait_ge(piece_loaded[p], c * 16 + 16 * (d * NC + 1))
                        if k == 1:
                            pe.wait_ge(h_done, PIECE * (p + 1) + 1)
                        else:
                            pe.wait_ge(split_ready, PIECE * (p + 1))
                        for i in range(PIECE):
                            a = p * PIECE + i
                            m = rows(a)
                            nodes = [hb[0:m, a, :]] if k == 1 else [splits[0:m, s, a, :] for s in range(3)]
                            for s, part in enumerate(nodes):
                                last = pe.matmul(bank[0][:, 0:w], part, pieces[d][0:m, p, i, 0:w],
                                                 start=(a == 0 and s == 0),
                                                 stop=(a == NB - 1 and s == len(nodes) - 1))
                        last.then_inc(piece_used, 1)
                        if p == PIECES - 1:
                            pe.wait_ge(piece_used, c * PIECES + (d * NC * PIECES + PIECES))
                            pe.sem_inc(dense_done, 1)
                    if b is not None:
                        pe.wait_ge(aT_ready, last_chunk + (d * NC + 1))
                        pe_products(pe, k, b, p * P, p % 2)

            chunk(0, CHUNK, None)
            if NFC > 1:
                with pe.Fori(0, NFC - 1) as c:
                    chunk(c + 1, CHUNK, c)
            chunk(NFC, NREST, NFC - 1)
            if k == 4:
                pe_turn_nodes(pe, k, NFULL)
            pe.wait_ge(aT_ready, (d + 1) * NC)
            pe_products(pe, k, NFULL)

        def pe_fast(pe):
            pe.wait_ge(fast_ready, 1)
            pe.sem_inc(seg_done, RING)
            pe.sem_inc(adj_done, OHRING)
            pe.sem_inc(prod_done, 1)
            pe.sem_inc(hs_T, 1)
            for k in range(PASSES):
                if k in GATHER:
                    pe_gather_pass(pe, k)
                else:
                    pe_dense_pass(pe, k)

        def pe_sum_general(pe, k):
            for n, (kk, first, relations, before) in enumerate(ROUNDS):
                if kk != k:
                    continue
                m = R2 if n == 0 else P
                a = g_types[:, :] if n == 0 else g_msg

                def tile(r, t, start, stop):
                    pe.wait_ge(g_oh, r * NT + t + (before + 1))
                    pe.wait_ge(g_gathered[n], (r * NT + t) * 16 + 16)
                    for c in range(NC):
                        last = pe.matmul(bank[c][0:m, :], a, wide[:, c, :], start=start, stop=stop)
                    last.then_inc(g_seg, 1)

                with pe.Fori(0, relations) as r:
                    tile(r, 0, True, False)
                    with pe.Fori(1, NT - 1) as t:
                        tile(r, t, False, False)
                    tile(r, NT - 1, False, True)

        def pe_transform(pe, k):
            aggs = by_relation(RELS[k])
            pe.wait_ge(agg_ready, k + 1)
            if k == 1:
                pe.wait_ge(wload[k], 16 * 2)
            for b in range(NB):
                m, n0 = rows(b), b * P
                if RELS[k] == R2:
                    if k * NB + b >= 2:
                        pe.wait_ge(tr_used, k * NB + b - 1)
                    for r in range(R2):
                        last = pe.matmul(bank[3 * (b % 2) + r // 4][0:m, (r % 4) * F:(r % 4 + 1) * F],
                                         aggs[:, r, n0:n0 + m], wts[:, r, :], start=True, stop=True)
                else:
                    if k * NB + b >= 2:
                        pe.wait_ge(tr_used, k * NB + b - 1)
                    for r in range(RELS[k]):
                        last = pe.matmul(bank[b % 2][0:m, 0:F], aggs[:, r, n0:n0 + m], wts[:, r, :],
                                         start=(r == 0), stop=(r == RELS[k] - 1))
                last.then_inc(tr_done, 1)
            if k == 0:
                for b in range(NB):
                    m = rows(b)
                    last = pe.transpose(bank[7][0:m, b * R2:(b + 1) * R2], counts[:, b * P:b * P + m],
                                        ident[0:R2, 0:R2])
                last.then_inc(cnt_T, 1)

        def pe_general(pe):
            roots = 0
            pe.sem_inc(g_seg, 1)
            for k in range(PASSES):
                if k >= 2:
                    pe_root(pe, roots, k)
                    roots += 1
                pe_sum_general(pe, k)
                pe_transform(pe, k)

        @block.tensor
        def _(pe):
            pe.wait_ge(good_ready, 1)
            pe.matmul(bank[7][0:1, 0:1], good[:, :], ones[:, :], start=True, stop=True).then_inc(flag_sum, 1)
            pe.wait_ge(flag_ok, 1)
            fast = pe.value_load(flag[0:1, 0:1], min_val=0, max_val=1)
            with pe.If(fast > 0):
                pe_fast(pe)
            with pe.Else():
                pe_general(pe)
            pe.nop()

        def dve_stats(dve, n, batch):
            b0 = batch * BATCH
            for b in range(b0, b0 + BATCH):
                m = rows(b)
                mark(dve.bn_stats(stats[0:m, b - b0, :], x[0:m, b, :]))
            meet()
            for b in range(b0, b0 + BATCH):
                m = rows(b)
                last = dve.bn_aggr(mv[0:m, b, :], stats[0:m, b - b0, :])
            last.then_inc(stats_ready, 1)
            dve.wait_ge(std_ready, n * NBATCH + batch + 1)
            link(dve.reciprocal(rstd[:, b0:b0 + BATCH], rstd[:, b0:b0 + BATCH]))
            dve.scalar_tensor_tensor(shift[:, b0:b0 + BATCH], mv[:, b0:b0 + BATCH, 0], -1.0,
                                     rstd[:, b0:b0 + BATCH], ALU.mult, ALU.mult).then_inc(scale_ready, 1)

        def dve_root(dve, n, k):
            dve.wait_ge(wload[k], 16 * 3)
            dve.wait_ge(table_ready, 16 * TABLE_DMAS * (k + 1))
            for b in range(NB):
                m = rows(b)
                dve.wait_ge(rt_mm, n * NB + b + 1)
                ps = bank[6 + b % 2][0:m, 0:F]
                if k == 3:
                    ins = dve.tensor_tensor(x[0:m, b, :], x[0:m, b, :], ps, ALU.add)
                    ins.then_inc(rt_used, 1)
                    dve.wait_ge(rt_used, n * NB + b + 1)
                    mark(dve.tensor_tensor(x[0:m, b, :], x[0:m, b, :], bias[0:m, :], ALU.add))
                else:
                    dve.tensor_tensor(hb[0:m, b, :], ps, bias[0:m, :], ALU.add).then_inc(rt_used, 1)
            meet()
            dve.wait_ge(rt_used, (n + 1) * NB)

        def dve_mix(dve):
            for c in range(NBASES):
                for r in range(R0):
                    s = comp[:, r * NBASES + c:r * NBASES + c + 1]
                    if c == 0:
                        mark(dve.tensor_scalar(wts[:, r, :], basis[:, c, :], s, None, ALU.mult))
                    else:
                        mark(dve.scalar_tensor_tensor(wts[:, r, :], basis[:, c, :], s, wts[:, r, :],
                                                      ALU.mult, ALU.add))
                meet()
            dve.sem_inc(mixed, 1)

        def dve_relations(dve):
            dve.wait_ge(logits_loaded, 16)
            link(dve.tensor_reduce(top, logits, X, ALU.max))
            link(dve.tensor_tensor(eq, logits, top.unsqueeze(2).broadcast_to([P, NT, R2]), ALU.is_equal))
            link(dve.tensor_tensor(eq, eq, down[:, :].unsqueeze(1).broadcast_to([P, NT, R2]), ALU.mult))
            link(dve.tensor_reduce(type10[:, 0:NT], eq, X, ALU.max))
            link(dve.tensor_scalar(type10[:, 0:NT], type10[:, 0:NT], -1.0, float(R2), ALU.mult, ALU.add))

        def dve_build(dve, k, g, slot):
            gi, n = GATHER[k], RELS[k] * WIN
            if k in COUNTS and slot % HALF == 0:
                h = (slot // HALF) % 2
                tiles = HALF * GT
                dve.wait_ge(seg_done, g + (gi * NG + HALF))
                dve.tensor_tensor(n_oh[:, h, :, :], iota[:, 0:WIN].unsqueeze(1).broadcast_to([P, tiles, WIN]),
                                  local[:, bass.ds(GT * g, tiles)].unsqueeze(2).broadcast_to([P, tiles, WIN]),
                                  ALU.is_equal)
                dve.tensor_tensor(t_oh[:, h, :, :], iota[:, 0:R2].unsqueeze(1).broadcast_to([P, tiles, R2]),
                                  type10[:, bass.ds(GT * g, tiles)].unsqueeze(2).broadcast_to([P, tiles, R2]),
                                  ALU.is_equal)
            dve.wait_ge(seg_done, g + (gi * NG + RING - OHRING + 1))
            for j in range(GT):
                c = bass.ds(GT * g + j, 1)
                o = oh[:, (slot * GT + j) % (OHRING * GT), 0:n]
                if WEIGHTED[k]:
                    last = dve.tensor_scalar(o, iota[:, 0:n], key[:, c], weight[:, c], ALU.is_equal, ALU.mult)
                else:
                    last = dve.tensor_scalar(o, iota[:, 0:n], key[:, c], None, ALU.is_equal)
            last.then_inc(oh_ready, 1)
            if k not in BUILDS:
                return
            ai = BUILDS[k]
            dve.wait_ge(adj_done, g + (ai * NG + 1))
            for j in range(GT):
                c = bass.ds(GT * g + j, 1)
                o = a_ohs[ai][:, (slot * GT + j) % (OHRING * GT), :]
                if ai == 0:
                    last = dve.tensor_scalar(o, iota[:, 0:NB * WIN], akey[:, c], weight[:, c],
                                             ALU.is_equal, ALU.mult)
                else:
                    last = dve.tensor_scalar(o, iota_h[:, :], akey[:, c], None, ALU.is_equal)
            last.then_inc(a_ready, 1)

        def dve_add(dve, k, g, u, place):
            gi = GATHER[k]
            dve.wait_ge(seg_done, g + (gi * NG + RING + 1))
            dve.wait_ge(acc_done, g + (gi * NG + BANKS))
            ps = bank[u % BANKS]
            slices = RELS[k] + (k in COUNTS)
            win = ring[:, 0:slices, bass.ds(place, WIN)]
            dve.tensor_tensor(win, win, ps[:, 0:slices * WIN].rearrange("p (r n) -> p r n", n=WIN),
                              ALU.add).then_inc(acc_done, 1)

        count = [0]

        def last_step(dve, q):
            dve.wait_ge(fin, q * FIN + count[0])

        def step_on(dve, q, ins):
            count[0] += 1
            ins.then_inc(fin, 1)
            last_step(dve, q)

        def close(dve):
            dve.sem_inc(fin, FIN - count[0])
            count[0] = 0

        def dve_fold(dve, k, b):
            q, n = b + k * NB, RELS[k] + (k in COUNTS)
            tail = ring[:, 0:n, SLOTS * P:SLOTS * P + WIN]
            dve.wait_ge(taken, b + (GATHER[k] * NB + 1))
            dve.scalar_tensor_tensor(S[:, 0:n, 0:WIN], tail, first_slot[:, bass.ds(b, 1)], S[:, 0:n, 0:WIN],
                                     ALU.mult, ALU.add).then_inc(S_ready, 1)
            dve.wait_ge(S_ready, b + (GATHER[k] * NB + 1))
            step_on(dve, q, dve.tensor_scalar(tail, tail, other_slot[:, bass.ds(b, 1)], None, ALU.mult))

        def dve_combine_fast(dve, k, b):
            m, q = rows(b), b + k * NB
            xb = block_of(x, b)[:, 0, :]
            one = bass.ds(b, 1)
            dve.wait_ge(prod_done, q + 2)
            if k == 0:
                ps = bank[7][0:m, 0:R2]
                dve.tensor_reduce(invdeg[0:m, one], ps, X, ALU.add)
                dve.tensor_scalar(inv10[0:m, one, :], ps.unsqueeze(1), 1.0, None, ALU.max)
                dve.tensor_tensor(xb, xb, bank[5][0:m, 0:F], ALU.add).then_inc(comb_done, 1)
                dve.wait_ge(comb_done, q + 2)
            elif k == 1:
                step_on(dve, q, dve.tensor_tensor(xb, xb, block_of(hb, b)[:, 0, :], ALU.add))
                step_on(dve, q, dve.tensor_tensor(xb, xb, root[0:m, :], ALU.add))
                dve.scalar_tensor_tensor(xb, bank[5][0:m, 0:F], adeg[0:m, one], xb,
                                         ALU.mult, ALU.add).then_inc(comb_done, 1)
                dve.wait_ge(comb_done, q + 2)
            elif k in GATHER:
                if k == 2:
                    dve.wait_ge(h_done, q + 1)
                step_on(dve, q, dve.tensor_tensor(acc[0:m, :], bank[7][0:m, 2 * F:3 * F], bias[0:m, :], ALU.add))
                for r in range(R2):
                    ins = dve.scalar_tensor_tensor(acc[0:m, :], bank[5 + r // 4][0:m, (r % 4) * F:(r % 4 + 1) * F],
                                                   inv10[0:m, one, r], acc[0:m, :], ALU.mult, ALU.add)
                    if r < R2 - 1:
                        step_on(dve, q, ins)
                ins.then_inc(comb_done, 1)
                dve.wait_ge(comb_done, q + 2)
                if k == 3:
                    step_on(dve, q, dve.tensor_tensor(xb, xb, acc[0:m, :], ALU.add))
            else:
                step_on(dve, q, dve.tensor_tensor(acc[0:m, :], bank[6][0:m, 0:F], bias[0:m, :], ALU.add))
                dve.scalar_tensor_tensor(acc[0:m, :], bank[5][0:m, 0:F], invdeg[0:m, one], acc[0:m, :],
                                         ALU.mult, ALU.add).then_inc(comb_done, 1)
                dve.wait_ge(comb_done, q + 2)
                dve.tensor_tensor_reduce(out=dist[0:m, 0, :], in0=acc[0:m, :], in1=acc[0:m, :], scale=1.0,
                                         scalar=0.0, op0=ALU.mult, op1=ALU.add,
                                         accum_out=f_sq[0:m, :]).then_inc(var_ready, 1)
            if k in (0, 1, 3):
                dve.sem_inc(dve_go, 1)
                step_on(dve, q, dve.bn_stats(stats[0:m, 0, :], xb))
                dve.wait_ge(h_done, q + 1)
                dve.sem_inc(dve_go, 1)
                dve.bn_aggr(f_mv[0:m, :], stats[0:m, 0, :]).then_inc(var_ready, 1)

        def dve_affine(dve, k, b):
            m, q = rows(b), b + k * NB
            dve.wait_ge(dev_ready, b + (NORMS[k] * NB + 1))
            if k == 4:
                step_on(dve, q, dve.tensor_scalar(f_inv[0:m, :], f_std[0:m, :], NORM_EPS, None, ALU.max))
                step_on(dve, q, dve.reciprocal(f_inv[0:m, :], f_inv[0:m, :]))
                xb = block_of(x, b)[:, 0, :]
                dve.scalar_tensor_tensor(xb, acc[0:m, :], f_inv[0:m, :], xb, ALU.mult, ALU.add).then_inc(x_done, 1)
                dve.wait_ge(x_done, b + 1)
            else:
                step_on(dve, q, dve.reciprocal(f_inv[0:m, :], f_std[0:m, :]))
                dve.scalar_tensor_tensor(f_shift[0:m, :], f_mv[0:m, 0:1], -1.0, f_inv[0:m, :],
                                         ALU.mult, ALU.mult).then_inc(affine_ready, 1)

        def dve_split(dve, k, b):
            m, q = rows(b), b + k * NB
            h = block_of(h2, b)[:, 0, :]
            part = [splits[0:m, s, bass.ds(b, 1), :][:, 0, :] for s in range(3)]
            dve.wait_ge(h_done, q + 2)
            dve.sem_inc(dve_go, 1)
            step_on(dve, q, dve.tensor_copy(part[0], h))
            step_on(dve, q, dve.tensor_tensor(acc[0:m, :], h, part[0], ALU.subtract))
            dve.sem_inc(dve_go, 1)
            step_on(dve, q, dve.tensor_copy(part[1], acc[0:m, :]))
            step_on(dve, q, dve.tensor_tensor(acc[0:m, :], acc[0:m, :], part[1], ALU.subtract))
            dve.sem_inc(dve_go, 1)
            dve.tensor_copy(part[2], acc[0:m, :]).then_inc(split_ready, 1)
            dve.wait_ge(split_ready, b + 1)

        def dve_gather_pass(dve, k):
            gi = GATHER[k]

            def finish(b, u):
                if u == 1 and k not in TAKEN_BY_ACT:
                    take(dve, k, b)
                if u == 3:
                    dve_fold(dve, k, b)
                if u == 6:
                    dve_combine_fast(dve, k, b)
                if u == 10 and k in NORMS:
                    dve_affine(dve, k, b)
                if u == 14:
                    dve.wait_ge(zeroed, b + (gi * NB + 1))
                    if k == 3:
                        dve_split(dve, k, b)
                    close(dve)

            def turns(g, n, b=None):
                places = [None] * n
                for u in range(n):
                    if u % AT_ONCE == 0:
                        places[u:u + AT_ONCE] = loads(ring_row, g + u, AT_ONCE, mybir.EngineType.DVE,
                                                      SLOTS * P - 1)
                    if b is not None:
                        finish(b, u)
                    dve_build(dve, k, g + u + LAG, u % RING + LAG)
                    dve_add(dve, k, g + u, u % RING, places[u])

            if gi:
                dve.wait_ge(oh_ready, gi * (NG + LAG))
            for g in range(LAG):
                dve_build(dve, k, g, g)
            for r in range(HEAD // RING):
                turns(RING * r, RING)
                if k == 0 and r == 0:
                    dve_mix(dve)
            with dve.Fori(0, NB - 2) as j:
                turns(BODY * j + HEAD, BODY, j)
            for b in range(NB - 2, NB):
                for u in range(BODY):
                    finish(b, u)

        def dve_dense_pass(dve, k):
            dve.wait_ge(wload[k], 16 * (2 if k == 1 else 3))
            if k == 1:
                link(dve.tensor_scalar(invdeg[:, :], invdeg[:, :], 1.0, None, ALU.max))
                mark(dve.reciprocal(inv10[:, :, :], inv10[:, :, :]))
                link(dve.reciprocal(invdeg[:, :], invdeg[:, :]))
                mark(dve.tensor_scalar(adeg[:, :], invdeg[:, :], alpha, None, ALU.mult))
                link(dve.tensor_scalar(root[:, :], bias[:, :], alpha, None, ALU.mult))

            def finish(b):
                dve_combine_fast(dve, k, b)
                dve_affine(dve, k, b)
                close(dve)

            with dve.Fori(0, NFC) as c:
                for i in range(SLOTS):
                    dve_combine_fast(dve, k, SLOTS * c + i)
                    dve_affine(dve, k, SLOTS * c + i)
                    close(dve)
            finish(NFULL)

        def dve_fast(dve):
            link(dve.tensor_copy(place_row[:, :], off_f[0:1, :]))
            link(dve.tensor_copy(carry_row[:, :], place_row[:, :]))
            starts_f = base_f[0:1, 0:NG].rearrange("p (i u) -> p i u", u=RING)[:, :, 0]
            link(dve.tensor_tensor(okb[0:1, 0:ITER - 1], starts_f[:, 1:], starts_f[:, 0:ITER - 1], ALU.subtract))
            link(dve.tensor_copy(carry_row[:, :].rearrange("p (i u) -> p i u", u=RING)[:, 1:, 0],
                                 okb[0:1, 0:ITER - 1]))
            link(dve.tensor_single_scalar(ring_row[:, :], base_row[:, 0:NG], SLOTS * P - 1, op=ALU.bitwise_and))
            link(dve.tensor_single_scalar(low_i, src[:, 0:NT], P - 1, op=ALU.bitwise_and))
            link(dve.tensor_copy(top, low_i))
            link(dve.tensor_scalar(neglo[:, 0:NT], top, -1.0, None, ALU.mult))
            link(dve.tensor_single_scalar(low_i, src[:, 0:NT], 7, op=ALU.logical_shift_right))
            link(dve.tensor_copy(hi_f, low_i))
            mark(dve.scalar_tensor_tensor(akey[:, 0:NT], hi_f, float(WIN), local[:, 0:NT], ALU.mult, ALU.add))
            mark(dve.scalar_tensor_tensor(key[:, 0:NT], type8_f, float(WIN), local[:, 0:NT], ALU.mult, ALU.add))
            for t in (neglo, akey, key, local, type10, weight):
                mark(dve.memset(t[:, NT:], 0.0))
            for k in COUNTS:
                for b in range(BANKS):
                    mark(dve.memset(bank[b][:, RELS[k] * WIN:(RELS[k] + 1) * WIN], 0.0))
            meet()
            dve.sem_inc(acc_done, BANKS)
            dve.sem_inc(comb_done, 1)
            dve.sem_inc(fast_ready, 1)
            dve.wait_ge(pool_prep, POOL_PREP)
            for k in range(PASSES):
                if k == 2:
                    link(dve.scalar_tensor_tensor(key[:, 0:NT], type10[:, 0:NT], float(WIN), local[:, 0:NT],
                                                  ALU.mult, ALU.add))
                if k in GATHER:
                    dve_gather_pass(dve, k)
                else:
                    dve_dense_pass(dve, k)

        def dve_sum_general(dve, k):
            for n, (kk, first, relations, before) in enumerate(ROUNDS):
                if kk != k:
                    continue
                rels_before = sum(x[2] for x in ROUNDS[:n])
                link(dve.memset(rel[:, :], float(first)))

                def tile(r, t):
                    c = bass.ds(t, 1)
                    dve.wait_ge(g_seg, r * NT + t + (before + 1))
                    ins = dve.tensor_tensor(g_key[:, :], local[:, c].broadcast_to([P, NC]), starts[:, :],
                                            ALU.subtract)
                    coef = None
                    if n == 0:
                        ins = dve.tensor_scalar(g_types[:, :], iota[:, 0:R2], type10[:, c], None, ALU.is_equal)
                    elif RELS[k] == 1:
                        coef = weight[:, c] if WEIGHTED[k] else None
                    else:
                        types = key if k == 0 else type10
                        coef = g_coef[:, :]
                        if WEIGHTED[k]:
                            ins = dve.tensor_scalar(coef, types[:, c], rel[:, :], weight[:, c],
                                                    ALU.is_equal, ALU.mult)
                        else:
                            ins = dve.tensor_scalar(coef, types[:, c], rel[:, :], None, ALU.is_equal)
                    ins.then_inc(g_step, 1)
                    dve.wait_ge(g_step, r * NT + t + (before + 1))
                    for q in range(NC):
                        if coef is None:
                            last = dve.tensor_scalar(wide[:, q, :], iota[:, :], g_key[:, q:q + 1], None,
                                                     ALU.is_equal)
                        else:
                            last = dve.tensor_scalar(wide[:, q, :], iota[:, :], g_key[:, q:q + 1], coef,
                                                     ALU.is_equal, ALU.mult)
                    last.then_inc(g_oh, 1)

                with dve.Fori(0, relations) as r:
                    with dve.Fori(0, NT) as t:
                        tile(r, t)
                    dve.wait_ge(g_seg, r * NT + (before + NT + 1))
                    for q in range(NC):
                        w = min(CHUNK, N - q * CHUNK)
                        if n == 0:
                            dve.tensor_copy(counts[:, q * CHUNK:q * CHUNK + w], bank[q][0:R2, 0:w])
                        else:
                            dve.tensor_copy(agg[:, bass.ds(r * N + (first * N + q * CHUNK), w)], bank[q][:, 0:w])
                    dve.tensor_scalar(rel[:, :], rel[:, :], 1.0, None, ALU.add).then_inc(g_rel, 1)
                    dve.wait_ge(g_rel, r + (rels_before + 1))
            dve.sem_inc(agg_ready, 1)

        def dve_combine(dve, k, b, n_norms):
            m, o = rows(b), b % 2
            dve.wait_ge(tr_done, k * NB + b + 1)
            xb, h = x[0:m, b, :], hb[0:m, b, :]
            if k == 0:
                dve.tensor_tensor(xb, xb, bank[o][0:m, 0:F], ALU.add).then_inc(tr_used, 1)
            elif k == 1:
                dve.scalar_tensor_tensor(xb, bank[o][0:m, 0:F], adeg[0:m, b:b + 1], xb,
                                         ALU.mult, ALU.add).then_inc(tr_used, 1)
            elif k in (2, 3):
                acc = h if k == 2 else xb
                for r in range(R2):
                    ps = bank[3 * o + r // 4][0:m, (r % 4) * F:(r % 4 + 1) * F]
                    ins = dve.scalar_tensor_tensor(acc, ps, inv10[0:m, b, r:r + 1], acc, ALU.mult, ALU.add)
                    if r < R2 - 1:
                        link(ins)
                ins.then_inc(tr_used, 1)
            else:
                dve.scalar_tensor_tensor(h, bank[o][0:m, 0:F], invdeg[0:m, b:b + 1], h,
                                         ALU.mult, ALU.add).then_inc(tr_used, 1)
                dve.wait_ge(tr_used, k * NB + b + 1)
                mark(dve.tensor_tensor_reduce(out=hT[0:m, b % 2, :], in0=h, in1=h, scale=1.0, scalar=0.0,
                                              op0=ALU.mult, op1=ALU.add, accum_out=shift[0:m, b:b + 1]))
                if b % BATCH < BATCH - 1:
                    return
                batch = b // BATCH
                b0 = batch * BATCH
                meet()
                dve.sem_inc(stats_ready, 1)
                dve.wait_ge(std_ready, n_norms * NBATCH + batch + 1)
                rn = rstd[:, b0:b0 + BATCH]
                link(dve.tensor_scalar(rn, rn, NORM_EPS, None, ALU.max))
                link(dve.reciprocal(rn, rn))
                for c in range(b0, b0 + BATCH):
                    mc = rows(c)
                    last = dve.scalar_tensor_tensor(x[0:mc, c, :], hb[0:mc, c, :], rstd[0:mc, c:c + 1],
                                                    x[0:mc, c, :], ALU.mult, ALU.add)
                last.then_inc(x_ready, 1)

        def dve_degrees(dve):
            dve.wait_ge(cnt_T, 1)
            parts = [(P, 0, NFULL), (NREST, NFULL, NB)]
            for m, b0, b1 in parts:
                ps = bank[7][0:m, b0 * R2:b1 * R2].rearrange("p (b r) -> p b r", r=R2)
                mark(dve.tensor_reduce(invdeg[0:m, b0:b1], ps, X, ALU.add))
                mark(dve.tensor_scalar(inv10[0:m, b0:b1, :], ps, 1.0, None, ALU.max))
            meet()
            link(dve.tensor_scalar(invdeg[:, :], invdeg[:, :], 1.0, None, ALU.max))
            mark(dve.reciprocal(inv10[:, :, :], inv10[:, :, :]))
            link(dve.reciprocal(invdeg[:, :], invdeg[:, :]))
            link(dve.tensor_scalar(adeg[:, :], invdeg[:, :], alpha[:, :], None, ALU.mult))

        def dve_skip(dve, k):
            dve.wait_ge(wload[k], 16 * 2)
            dve.wait_ge(h_ready, (k + 1) * NBATCH)
            link(dve.tensor_scalar(root[:, :], bias[:, :], alpha[:, :], None, ALU.mult))
            for m, b0, b1 in [(P, 0, NFULL), (NREST, NFULL, NB)]:
                mark(dve.tensor_tensor(x[0:m, b0:b1, :], x[0:m, b0:b1, :], hb[0:m, b0:b1, :], ALU.add))
            meet()
            for m, b0, b1 in [(P, 0, NFULL), (NREST, NFULL, NB)]:
                mark(dve.tensor_tensor(x[0:m, b0:b1, :], x[0:m, b0:b1, :],
                                       root[0:m, :].unsqueeze(1).broadcast_to([m, b1 - b0, F]), ALU.add))
            meet()

        def dve_general(dve):
            norms = roots = 0
            for k in range(PASSES):
                for batch in range(NBATCH):
                    if k:
                        for b in range(batch * BATCH, (batch + 1) * BATCH):
                            dve_combine(dve, k - 1, b, norms)
                        dve.wait_ge(tr_used, (k - 1) * NB + (batch + 1) * BATCH)
                    if k and k != 3:
                        dve_stats(dve, norms, batch)
                norms += k != 3
                if k == 1:
                    dve_degrees(dve)
                    dve_skip(dve, k)
                if k >= 2:
                    dve_root(dve, roots, k)
                    roots += 1
                dve_sum_general(dve, k)
            for b in range(NB):
                dve_combine(dve, PASSES - 1, b, norms)

        @block.vector
        def _(dve):
            for t, v in ((mv, 0.0), (eps, LN_EPS), (ones, 1.0), (zero, 0.0), (shift, 0.0), (invdeg, 1.0),
                         (inv10, 1.0), (checks, 0.0)):
                mark(dve.memset(t, v) if t in (eps, ones, zero) else dve.memset(t[:], v))
            for q in range(NC):
                mark(dve.memset(starts[:, q:q + 1], float(q * CHUNK)))
            dve.wait_ge(x_loaded, 16 * 2)
            for batch in range(NBATCH):
                dve_stats(dve, 0, batch)
            dve.wait_ge(loaded, 16 * LOADS)
            mark(dve.tensor_copy(dst_f, dst_i))
            mark(dve.tensor_copy(base_f, base_i))
            link(dve.tensor_copy(type8_f, type8_i))
            base = base_f[:, 0:NG]

            def by_group(t):
                return t.rearrange("p (g t) -> p g t", t=GT)

            link(dve.tensor_tensor(by_group(local[:, 0:NT]), by_group(dst_f),
                                   base.unsqueeze(2).broadcast_to([P, NG, GT]), ALU.subtract))
            link(dve.tensor_scalar(top, local[:, 0:NT], 0.0, None, ALU.is_ge))
            link(dve.scalar_tensor_tensor(top, local[:, 0:NT], float(WIN), top, ALU.is_lt, ALU.mult))
            link(dve.tensor_tensor(by_group(hi_f), by_group(dst_f),
                                   base_f[:, 1:].unsqueeze(2).broadcast_to([P, NG, GT]), ALU.is_le))
            link(dve.tensor_tensor(top, top, hi_f, ALU.mult))
            n = NT - GT
            link(dve.tensor_tensor(hi_f[:, 0:n], dst_f[:, 0:n], dst_f[:, GT:], ALU.is_lt))
            link(dve.tensor_tensor(top[:, 0:n], top[:, 0:n], hi_f[:, 0:n], ALU.mult))
            link(dve.scalar_tensor_tensor(top, dst_f, float(PAD_DST), top, ALU.is_ge, ALU.max))
            mark(dve.tensor_reduce(checks[:, 0:1], top, X, ALU.add))
            link(dve.tensor_tensor(off_f, base_f[:, 1:], base, ALU.subtract))
            link(dve.tensor_scalar(okb, off_f, float(WIN - 1), None, ALU.is_le))
            dve.wait_ge(pool_prep, 3)
            link(dve.scalar_tensor_tensor(off_f, iota[:, 0:NG], -float(STEP), base, ALU.mult, ALU.add))
            link(dve.scalar_tensor_tensor(okb, off_f, -float(LATE), okb, ALU.is_ge, ALU.mult))
            link(dve.scalar_tensor_tensor(okb, off_f, float(EARLY), okb, ALU.is_le, ALU.mult))
            link(dve.tensor_tensor(off_f.rearrange("p (i u) -> p i u", u=RING),
                                   base.rearrange("p (i u) -> p i u", u=RING),
                                   base.rearrange("p (i u) -> p i u", u=RING)[:, :, 0:1].broadcast_to(
                                       [P, ITER, RING]), ALU.subtract))
            link(dve.scalar_tensor_tensor(okb, off_f, float(CAP - WIN), okb, ALU.is_le, ALU.mult))
            link(dve.scalar_tensor_tensor(okb[:, 0:1], base[:, 0:1], 0.0, okb[:, 0:1], ALU.is_equal, ALU.mult))
            link(dve.tensor_reduce(checks[:, 1:2], okb, X, ALU.add))
            dve.tensor_tensor(good[:, :], checks[:, 0:1], checks[:, 1:2], ALU.add).then_inc(good_ready, 1)
            dve.wait_ge(flag_sum, 1)
            dve.tensor_scalar(flag[:, :], bank[7][0:1, 0:1], P * (NT + NG) - 0.5, None,
                              ALU.is_ge).then_inc(flag_ok, 1)
            link(dve.tensor_scalar(down[:, :], iota[:, 0:R2], -1.0, float(R2), ALU.mult, ALU.add))
            dve_relations(dve)
            dve.wait_ge(flag_ok, 1)
            fast = dve.value_load(flag[0:1, 0:1], min_val=0, max_val=1)
            steps = step[0]
            with dve.If(fast > 0):
                dve_fast(dve)
            with dve.Else():
                step[0] = steps
                dve.wait_ge(pool_prep, POOL_PREP)
                dve_mix(dve)
                mark(dve.tensor_copy(key[:, 0:NT], type8_f))
                link(dve.tensor_copy(local[:, 0:NT], dst_f))
                dve_general(dve)
            dve.nop()


def _layout(inputs):
    import numpy as np
    a = {n: np.asarray(v) for n, v in inputs.items()}
    E = a["src"].shape[0]
    group = GT * P
    NG = -(-E // (group * RING)) * RING
    NT = NG * GT

    def tiled(v, fill):
        full = np.full((NT * P,) + v.shape[1:], fill, v.dtype)
        full[:E] = v
        return np.ascontiguousarray(np.moveaxis(full.reshape((NT, P) + v.shape[1:]), 0, 1))

    firsts = a["dst"][::group]
    base = np.full(NG + 1, a["x"].shape[0] - 1, firsts.dtype)
    base[:len(firsts)] = firsts
    return {
        "x": a["x"],
        "src": tiled(a["src"], 0),
        "dst": tiled(a["dst"], PAD_DST),
        "base": base,
        "type8": tiled(a["edge_type_8"], 0),
        "logits": tiled(a["edge_attr_42"][:, EMB:-EMB], 0),
        "weight": tiled(a["edge_weight"], 0),
        "comp": a["L0_gnn_w_comp"].reshape(-1),
        "bases": a["L0_gnn_bases"],
        "w1t": np.ascontiguousarray(a["L1_gnn_W"].T),
        "b1": a["L1_gnn_b"],
        "alpha": a["L1_gnn_alpha"].reshape(1),
        "wrel_a": a["L2_gnn_w_rel1"].reshape(-1, F),
        "root_a": a["L2_gnn_root1"],
        "bias_a": a["L2_gnn_b1"],
        "wrel_b": a["L2_gnn_w_rel2"].reshape(-1, F),
        "root_b": a["L2_gnn_root2"],
        "bias_b": a["L2_gnn_b2"],
        "w3rel": np.ascontiguousarray(a["L3_gnn_W_rel"].T),
        "b3": a["L3_gnn_b_rel"],
        "w3root": np.ascontiguousarray(a["L3_gnn_W_root"].T),
    }


def kernel(**inputs):
    import concourse.bacc as _bacc
    from concourse import mybir as _mybir
    from concourse.bass_utils import run_bass_kernel_spmd as _run

    nc = _bacc.Bacc("TRN2", target_bir_lowering=False, num_devices=1)
    arrays, args = {}, []
    for name, a in _layout(inputs).items():
        arrays[f"in_{name}"] = a
        args.append(nc.dram_tensor(f"in_{name}", a.shape, _mybir.dt.from_np(a.dtype), kind="ExternalInput").ap())
    shape = inputs["x"].shape
    args.append(nc.dram_tensor("out_0", shape, _mybir.dt.float32, kind="ExternalOutput").ap())
    graph_layers(nc, *args)
    r = _run(nc, [arrays], core_ids=[0])
    return r.results[0]["out_0"]
```
